# Optimizing a Trainium2 kernel written in Bass

```python
import numpy as np
import jax
import jax.numpy as jnp

def _softmax(x, axis=-1):
    return jax.nn.softmax(x, axis=axis)
def _gelu(x):
    return jax.nn.gelu(x, approximate=True)
def _silu(x):
    return jax.nn.silu(x)
def _sigmoid(x):
    return jax.nn.sigmoid(x)
def _layernorm(x, axis=-1, eps=1e-5):
    m = jnp.mean(x, axis=axis, keepdims=True)
    v = jnp.var(x, axis=axis, keepdims=True)
    return (x - m) / jnp.sqrt(v + eps)
def _scatter_add(tgt, idx, src, axis=0):
    return tgt.at[idx].add(src)
def _segment_sum(src, seg, n):
    return jax.ops.segment_sum(src, seg, n)

kernel_name = 'mk_adj_resnorm_d4_adj_128_c6311c'

def setup_inputs(seed: int = 0):
    np.random.seed(seed)
    _w = jnp.asarray
    def _rec_inputs():
        import jax
        import jax.numpy as jnp
        _gk = jax.random.key(seed)
        x = -0.003407 + 1.001 * jax.random.normal(jax.random.fold_in(_gk, 1), (3327, 128), jnp.float32)
        _w = (1.0 + jnp.arange(3327, dtype=jnp.float32)) ** -0.5
        _w = _w / _w.mean()
        _pij = jnp.clip(0.00240457 * _w[:, None] * _w[None, :], 0.0, 1.0)
        _a = jax.random.uniform(jax.random.fold_in(_gk, 2), (3327, 3327)) < _pij
        _a = jnp.logical_or(_a, jnp.swapaxes(_a, -1, -2))
        _a = jnp.logical_or(_a, jnp.eye(3327, dtype=bool))
        _af = _a.astype(jnp.float32)
        _af = _af * jax.random.uniform(jax.random.fold_in(_gk, 3), (3327, 3327), jnp.float32, 0.05, 5.06092)
        adj = _af
        return x, adj
    x, adj = _rec_inputs()
    def _L0_gnn_setup():
        import jax, jax.numpy as jnp
        import numpy as np
        N = 1024
        D = 128
        H = 8
        key = jax.random.key(seed)
        ks = jax.random.split(key, 7)
        s = (D * H) ** (-0.5)
        return {'x': jax.random.normal(ks[0], (N, D), dtype=jnp.float32), 'spatial_encoding': jax.random.normal(ks[1], (N, N), dtype=jnp.float32), 'edge_encoding': jax.random.normal(ks[2], (N, N), dtype=jnp.float32), 'Wq': jax.random.normal(ks[3], (D * H, D), dtype=jnp.float32) * s, 'Wk': jax.random.normal(ks[4], (D * H, D), dtype=jnp.float32) * s, 'Wv': jax.random.normal(ks[5], (D * H, D), dtype=jnp.float32) * s, 'Wo': jax.random.normal(ks[6], (D, D * H), dtype=jnp.float32) * s}
    _L0_gnn_all = _L0_gnn_setup()
    _L0_gnn_in = {k: v for k, v in _L0_gnn_all.items() if k in ('Wq', 'Wk', 'Wv', 'Wo', )}
    del _L0_gnn_all

    def _L1_gnn_setup():
        import jax, jax.numpy as jnp
        import numpy as np
        N = 8192
        D = 128
        EDGE_P = 0.005
        key = jax.random.key(seed)
        kx, ka, kb = jax.random.split(key, 3)
        x = jax.random.normal(kx, (N, D), dtype=jnp.float32)
        adj = (jax.random.uniform(ka, (N, N)) < EDGE_P).astype(jnp.float32)
        adj = jnp.maximum(adj, jnp.eye(N, dtype=jnp.float32))
        beta = jax.random.uniform(kb, (1,), dtype=jnp.float32)
        return {'x': x, 'adj': adj, 'beta': beta}
    _L1_gnn_all = _L1_gnn_setup()
    _L1_gnn_in = {k: v for k, v in _L1_gnn_all.items() if k in ('beta', )}
    del _L1_gnn_all

    def _L2_gnn_setup():
        import jax, jax.numpy as jnp
        import numpy as np
        N = 16384
        U = 128
        AVG_DEGREE = 32
        key = jax.random.key(seed)
        kx, ka, kw = jax.random.split(key, 3)
        x = jax.random.normal(kx, (N, U), dtype=jnp.float32)
        adj = (jax.random.uniform(ka, (N, N)) < AVG_DEGREE / N).astype(jnp.float32)
        W = jax.random.normal(kw, (U, U), dtype=jnp.float32) * 0.05
        b = jnp.zeros((U,), dtype=jnp.float32)
        return {'x': x, 'adj': adj, 'W': W, 'b': b}
    _L2_gnn_all = _L2_gnn_setup()
    _L2_gnn_in = {k: v for k, v in _L2_gnn_all.items() if k in ('W', 'b', )}
    del _L2_gnn_all

    def _L3_gnn_setup():
        import jax, jax.numpy as jnp
        import numpy as np

        def _lap_mul(A, x):
            d = 1.0 / jnp.sqrt(jnp.sum(A, axis=-1))
            return d[:, None] * (A @ (d[:, None] * x))
        key = jax.random.key(seed)
        k1, k2, k3, k4, k5, k6 = jax.random.split(key, 6)
        N, D_IN, D_OUT = (4096, 128, 128)
        x = jax.random.normal(k1, (N, D_IN), dtype=jnp.float32)
        A = jax.random.uniform(k2, (N, N), dtype=jnp.float32)
        s1 = 1.0 / np.sqrt(D_IN)
        W1 = jax.random.uniform(k3, (D_IN, D_OUT), minval=-s1, maxval=s1, dtype=jnp.float32)
        b1 = jax.random.uniform(k4, (D_OUT,), minval=-s1, maxval=s1, dtype=jnp.float32)
        W2 = jax.random.uniform(k5, (D_IN, D_OUT), minval=-s1, maxval=s1, dtype=jnp.float32)
        b2 = jax.random.uniform(k6, (D_OUT,), minval=-s1, maxval=s1, dtype=jnp.float32)
        return {'x': x, 'A': A, 'W1': W1, 'b1': b1, 'W2': W2, 'b2': b2, 'sigma': 1, 'k': 4}
    _L3_gnn_all = _L3_gnn_setup()
    _L3_gnn_in = {k: v for k, v in _L3_gnn_all.items() if k in ('W1', 'b1', 'W2', 'b2', )}
    del _L3_gnn_all

    return {
        "x": x,
        "adj": adj,
        "L0_gnn_Wq": _L0_gnn_in["Wq"],
        "L0_gnn_Wk": _L0_gnn_in["Wk"],
        "L0_gnn_Wv": _L0_gnn_in["Wv"],
        "L0_gnn_Wo": _L0_gnn_in["Wo"],
        "L1_gnn_beta": _L1_gnn_in["beta"],
        "L2_gnn_W": _L2_gnn_in["W"],
        "L2_gnn_b": _L2_gnn_in["b"],
        "L3_gnn_W1": _L3_gnn_in["W1"],
        "L3_gnn_b1": _L3_gnn_in["b1"],
        "L3_gnn_W2": _L3_gnn_in["W2"],
        "L3_gnn_b2": _L3_gnn_in["b2"],
    }

def reference(x, adj, L0_gnn_Wq, L0_gnn_Wk, L0_gnn_Wv, L0_gnn_Wo, L1_gnn_beta, L2_gnn_W, L2_gnn_b, L3_gnn_W1, L3_gnn_b1, L3_gnn_W2, L3_gnn_b2):
    import jax
    import jax.numpy as jnp
    def _L0_gnn_ref(x, spatial_encoding, edge_encoding, Wq, Wk, Wv, Wo):
        import jax, jax.numpy as jnp
        import numpy as np
        N = 1024
        D = 128
        H = 8
        n, d = x.shape
        h = Wq.shape[0] // d
        scale = d ** (-0.5)
        q = (x @ Wq.T).reshape(d, n, h)
        k = (x @ Wk.T).reshape(d, n, h)
        v = (x @ Wv.T).reshape(d, n, h)
        a = jnp.einsum('dnh,dmh->dnm', q, k) * scale
        a = a + spatial_encoding + edge_encoding
        a = jax.nn.softmax(a, axis=2)
        out = jnp.einsum('dnm,dmh->dnh', a, v)
        out = out.reshape(n, h * d)
        return out @ Wo.T

    def _L1_gnn_ref(x, adj, beta):
        import jax, jax.numpy as jnp
        import numpy as np
        N = 8192
        D = 128
        EDGE_P = 0.005
        norm2 = jnp.linalg.norm(x, axis=1, keepdims=True)
        cos = beta[0] * (x @ x.T) / (norm2 @ norm2.T + 1e-07)
        masked = cos + (1.0 - adj) * -1000000000.0
        P = jax.nn.softmax(masked, axis=1)
        return P @ x

    def _L2_gnn_ref(x, adj, W, b):
        import jax, jax.numpy as jnp
        import numpy as np
        N = 16384
        U = 128
        AVG_DEGREE = 32
        adj = jax.lax.stop_gradient(adj)
        neigh1 = adj @ x
        x1 = jax.nn.swish(neigh1 @ W + b)
        neigh2 = adj @ x1
        x2 = jax.nn.swish(neigh2 @ W + b)
        return x2

    def _L3_gnn_ref(x, A, W1, b1, W2, b2, sigma, k):
        import jax, jax.numpy as jnp
        import numpy as np

        def _lap_mul(A, x):
            d = 1.0 / jnp.sqrt(jnp.sum(A, axis=-1))
            return d[:, None] * (A @ (d[:, None] * x))
        z = _lap_mul(A, x) @ W1 + b1
        z = jax.nn.leaky_relu(z, negative_slope=0.1)
        sq = jnp.sum(z * z, axis=-1)
        d2 = sq[:, None] + sq[None, :] - 2.0 * (z @ z.T)
        d2 = jnp.maximum(d2, 0.0)
        S = jnp.sqrt(d2 + 1e-10)
        S = jnp.exp(-S / (2.0 * sigma))
        order = jnp.argsort(-S, axis=-1)
        ranks = jnp.argsort(order, axis=-1)
        S = jnp.where(ranks < k, S, 0.0)
        A2 = S + A
        out = _lap_mul(A2, x) @ W2 + b2
        return out

    x = _layernorm(x + _L0_gnn_ref(x, adj, adj, L0_gnn_Wq, L0_gnn_Wk, L0_gnn_Wv, L0_gnn_Wo), axis=-1)
    x = _layernorm(x + _L1_gnn_ref(x, adj, L1_gnn_beta), axis=-1)
    x = _layernorm(x + _L2_gnn_ref(x, adj, L2_gnn_W, L2_gnn_b), axis=-1)
    x = _layernorm(x + _L3_gnn_ref(x, adj, L3_gnn_W1, L3_gnn_b1, L3_gnn_W2, L3_gnn_b2, 1, 4), axis=-1)
    return x


_drawn_inputs = setup_inputs


def setup_inputs(seed=0):
    import zlib

    import numpy as np

    out = dict(_drawn_inputs(seed))
    spreads = {'L2_gnn_b': (0.0, 0.425)}
    factors = {'L0_gnn_Wq': 8.0, 'L0_gnn_Wk': 8.0, 'L3_gnn_W1': 6.062, 'L3_gnn_b1': 8.0}
    for name, (base, spread) in spreads.items():
        noise = np.random.default_rng([zlib.crc32(name.encode()), seed]).standard_normal(out[name].shape)
        drawn = base * np.exp(spread * noise) if base else spread * noise
        out[name] = jnp.asarray(drawn.astype(out[name].dtype))
    for name, factor in factors.items():
        out[name] = (out[name] * factor).astype(out[name].dtype)
    return out
```

```python
import concourse.bass as bass
from concourse import mybir
from contextlib import ExitStack

fp32 = mybir.dt.float32
bf16 = mybir.dt.bfloat16
ALU = mybir.AluOpType
ACT = mybir.ActivationFunctionType
AX = mybir.AxisListType

N, D = 3327, 128
HEADS, C = 128, 8
FEAT = HEADS * C
G = N * HEADS
RT = -(-N // 128)
LAST = N - 128 * (RT - 1)
LOWEST = -3.0e38


def width(t):
    return 128 if not isinstance(t, int) or t < RT - 1 else LAST


def after(t, n):
    return not isinstance(t, int) or t >= n


def tiles(eng, body, end=RT):
    for t in range(2):
        body(t, t % 2)
    with eng.Fori(1, RT // 2 - 1) as pair:
        for p in range(2):
            body(pair * 2 + p, p)
    for t in range(RT - 2, end):
        body(t, t % 2)


def count(t, p, each=16):
    return (t - p) * (each // 2) + each


def node_rows(t):
    return bass.ds(t * 128, width(t))


def at(t):
    return t if isinstance(t, int) else bass.ds(t, 1)


def row_of(buffer, t):
    n = width(t)
    if isinstance(t, int):
        return buffer[0:n, t, :]
    return buffer[:, bass.ds(t, 1), :].rearrange("p o n -> p (o n)")


def banks(n, size=512):
    return [(a, min(size, n - a)) for a in range(0, n, size)]


def write_identity(nc, pool, ident, done):
    pool.memset(ident[:, :], 0.0).then_inc(done, 1)
    pool.wait_ge(done, 1)
    pool.affine_select(out=ident[:, :], in_=ident[:, :], compare_op=ALU.not_equal, fill=1.0, base=0,
                       pattern=[[-1, 128]], channel_multiplier=1).then_inc(done, 1)


def project(nc, sem, x, Wq, Wk, Wv, q_planes, k_planes, v_planes):
    Q_SCALE = 0.5 * float(D) ** -0.5
    with ExitStack() as ctx:
        def sb(name, shape, dt=fp32):
            return ctx.enter_context(nc.sbuf_tensor(name, shape, dt))

        x_in = sb("p_x_in", [128, 2, D])
        w_in = sb("p_w_in", [128, 3, C, D])
        w_t = sb("p_w_t", [128, 3, C, 128])
        xt = sb("p_xt", [128, 2, 128])
        ident = sb("p_ident", [128, 128])
        full = sb("p_full", [128, 2, 3, FEAT])
        rest = sb("p_rest", [128, 2, FEAT])
        part = sb("p_part", [128, 2, 2, 3, FEAT], bf16)
        turn = ctx.enter_context(nc.psum_tensor("p_turn", [128, 2, 512], fp32))
        proj = ctx.enter_context(nc.psum_tensor("p_proj", [128, 3, 2, 512], fp32))

        ident_made = sem("p_ident_made")
        w_loaded = sem("p_w_loaded")
        x_loaded = [sem(f"p_x_loaded{i}") for i in range(2)]
        w_turned = sem("p_w_turned")
        w_copied = sem("p_w_copied")
        x_turned = sem("p_x_turned")
        x_copied = sem("p_x_copied")
        projected = sem("p_projected")
        taken = sem("p_taken")
        q_split = sem("p_q_split")
        k_split = sem("p_k_split")
        stored = [sem(f"p_stored{i}") for i in range(2)]
        passed_dve, passed_pool = sem("p_passed_dve"), sem("p_passed_pool")
        passed_sp = sem("p_passed_sp")

        PARTS = 5
        STORES = 16 * 7
        block = ctx.enter_context(nc.Block())

        @block.sync
        def _(sp):
            for m, w in enumerate((Wq, Wk, Wv)):
                sp.dma_start(w_in[:, m], w.rearrange("(j c) d -> j c d", c=C)).then_inc(w_loaded, 16)

            def store(t, p):
                n = width(t)
                rows = bass.ds(t * (128 * 128), n * 128)
                sp.wait_ge(taken, t * 3 + 3)
                sp.sem_inc(passed_sp, 1)
                sp.dma_start(v_planes[:, rows].rearrange("c (m j) -> m c j", j=128),
                             full[0:n, p, 2].rearrange("m (c j) -> m c j", c=C)).then_inc(stored[p], 16)
                for m, (planes, split) in enumerate(((q_planes, q_split), (k_planes, k_split))):
                    sp.wait_ge(split, t * PARTS + PARTS)
                    sp.sem_inc(passed_sp, 1)
                    for s in range(3):
                        sp.dma_start(planes[s, :, rows].rearrange("c (m j) -> m c j", j=128),
                                     part[0:n, p, m, s].rearrange("m (c j) -> m c j", c=C)) \
                            .then_inc(stored[p], 16)

            def body(t, p):
                if after(t, 2):
                    sp.wait_ge(x_turned, t - 1)
                    sp.sem_inc(passed_sp, 1)
                sp.dma_start(x_in[0:width(t), p], x[node_rows(t)]).then_inc(x_loaded[p], 16)
                if after(t, 1):
                    store(t - 1, 1 - p)

            tiles(sp, body)
            store(RT - 1, 1)
            for p in range(2):
                sp.wait_ge(stored[p], STORES * RT // 2)

        @block.tensor
        def _(pe):
            pe.wait_ge(ident_made, 2)
            pe.wait_ge(w_loaded, 48)
            for i in range(6):
                m, c0 = i // 2, 4 * (i % 2)
                if i >= 2:
                    pe.wait_ge(w_copied, i - 1)
                for c in range(4):
                    mm = pe.transpose(turn[:, i % 2, c * 128:c * 128 + 128], w_in[:, m, c0 + c], ident[:, :])
                mm.then_inc(w_turned, 1)
            pe.wait_ge(w_copied, 6)

            def body(t, p):
                n = width(t)
                pe.wait_ge(x_loaded[p], count(t, p))
                if after(t, 2):
                    pe.wait_ge(x_copied, t - 1)
                pe.transpose(turn[:, p, 0:n], x_in[0:n, p], ident[0:n, 0:n]).then_inc(x_turned, 1)
                pe.wait_ge(x_copied, t + 1)
                for m in range(3):
                    if after(t, 1):
                        pe.wait_ge(taken, t * 3 + (m - 2))
                    for b in range(2):
                        mm = pe.matmul(proj[0:n, m, b], xt[:, p, 0:n],
                                       w_t[:, m, 4 * b:4 * b + 4].rearrange("d c j -> d (c j)"),
                                       start=True, stop=True)
                    mm.then_inc(projected, 1)

            tiles(pe, body)

        @block.scalar
        def _(act):
            def body(t, p):
                n = width(t)
                for m, scale in enumerate((Q_SCALE, 1.0, 1.0)):
                    act.wait_ge(projected, t * 3 + (m + 1))
                    if after(t, 2) and m == 0:
                        act.wait_ge(stored[p], count(t - 2, p, STORES))
                        act.wait_ge(q_split, t * PARTS - PARTS)
                        act.wait_ge(k_split, t * PARTS - PARTS)
                    act.activation(full[0:n, p, m], proj[0:n, m].rearrange("m b c -> m (b c)"),
                                   ACT.Copy, scale=scale).then_inc(taken, 1)

            tiles(act, body)

        def split(eng, m, done, passed, t, p):
            n = width(t)
            src, left, out = full[0:n, p, m], rest[0:n, m], part[0:n, p, m]
            eng.wait_ge(taken, t * 3 + (m + 1))
            eng.sem_inc(passed, 1)
            if after(t, 2):
                eng.wait_ge(stored[p], count(t - 2, p, STORES))
                eng.sem_inc(passed, 1)
            steps = [lambda: eng.tensor_copy(out[:, 0], src),
                     lambda: eng.tensor_tensor(left, src, out[:, 0], ALU.subtract),
                     lambda: eng.tensor_copy(out[:, 1], left),
                     lambda: eng.tensor_tensor(left, left, out[:, 1], ALU.subtract),
                     lambda: eng.tensor_copy(out[:, 2], left)]
            for i, step in enumerate(steps):
                step().then_inc(done, 1)
                eng.wait_ge(done, t * PARTS + (i + 1))
                eng.sem_inc(passed, 1)

        @block.vector
        def _(dve):
            for i in range(6):
                dve.wait_ge(w_turned, i + 1)
                m, c0 = i // 2, 4 * (i % 2)
                dve.tensor_copy(w_t[:, m, c0:c0 + 4].rearrange("d c j -> d (c j)"), turn[:, i % 2]) \
                    .then_inc(w_copied, 1)

            def body(t, p):
                n = width(t)
                dve.wait_ge(x_turned, t + 1)
                if after(t, 2):
                    dve.wait_ge(projected, t * 3 - 3)
                dve.tensor_copy(xt[:, p, 0:n], turn[:, p, 0:n]).then_inc(x_copied, 1)
                split(dve, 0, q_split, passed_dve, t, p)

            tiles(dve, body)

        @block.gpsimd
        def _(pool):
            write_identity(nc, pool, ident, ident_made)
            tiles(pool, lambda t, p: split(pool, 1, k_split, passed_pool, t, p))


V_ROW = RT * (C + 1)


def lay_out_values(nc, sem, v_planes, v_tiles):
    HG = 128 // C
    GROUPS = HEADS // HG
    with ExitStack() as ctx:
        planes = ctx.enter_context(nc.sbuf_tensor("v_planes_in", [128, 2, N], fp32))
        tiles = ctx.enter_context(nc.sbuf_tensor("v_tiles_out", [128, 2, HG, RT, C + 1], fp32))
        ident = ctx.enter_context(nc.sbuf_tensor("v_ident", [128, 128], fp32))
        turn = ctx.enter_context(nc.psum_tensor("v_turn", [128, 4, 512], fp32))
        ident_made, turned = sem("v_ident_made"), sem("v_turned")
        loaded = [sem(f"v_loaded{i}") for i in range(2)]
        copied, ones_made = sem("v_copied"), sem("v_ones_made")
        stored = [sem(f"v_stored{i}") for i in range(2)]
        block = ctx.enter_context(nc.Block())

        def store(sp, g):
            sp.wait_ge(copied, RT * (g + 1))
            sp.wait_ge(ones_made, 1)
            sp.dma_start(v_tiles[g * HG:g * HG + HG].rearrange("h p n -> p h n"),
                         tiles[:, g % 2].rearrange("p h t c -> p h (t c)")).then_inc(stored[g % 2], 16)

        @block.sync
        def _(sp):
            for g in range(GROUPS):
                if g >= 2:
                    sp.wait_ge(turned, RT * (g - 1))
                for h in range(HG):
                    start = (g * HG + h) * N
                    sp.dma_start(planes[h * C:h * C + C, g % 2], v_planes[:, start:start + N]) \
                        .then_inc(loaded[g % 2], 16)
                if g >= 1:
                    store(sp, g - 1)
            store(sp, GROUPS - 1)
            for p in range(2):
                sp.wait_ge(stored[p], 16 * GROUPS // 2)

        @block.gpsimd
        def _(pool):
            write_identity(nc, pool, ident, ident_made)

        @block.tensor
        def _(pe):
            pe.wait_ge(ident_made, 2)
            for g in range(GROUPS):
                pe.wait_ge(loaded[g % 2], 16 * HG * (g // 2 + 1))
                for t in range(RT):
                    u = g * RT + t
                    if u >= 4:
                        pe.wait_ge(copied, u - 3)
                    pe.transpose(turn[0:width(t), u % 4, 0:128], planes[:, g % 2, t * 128:t * 128 + width(t)],
                                 ident[:, :]).then_inc(turned, 1)

        @block.vector
        def _(dve):
            dve.memset(tiles[:, :, :, :, :].rearrange("p b h t c -> p (b h t c)"), 1.0).then_inc(ones_made, 1)
            dve.wait_ge(ones_made, 1)
            for g in range(GROUPS):
                if g >= 2:
                    dve.wait_ge(stored[g % 2], 16 * (g // 2))
                for t in range(RT):
                    u = g * RT + t
                    dve.wait_ge(turned, u + 1)
                    dve.tensor_copy(tiles[0:width(t), g % 2, :, t, 0:C],
                                    turn[0:width(t), u % 4, 0:128].rearrange("p (h c) -> p h c", c=C)) \
                        .then_inc(copied, 1)


CHUNKS = 7
CSTEP = 475
CHUNK = N - (CHUNKS - 1) * CSTEP
assert CSTEP <= CHUNK <= 512
SUBS = [(a, min(120, CHUNK - a)) for a in range(0, CHUNK, 120)]
KROWS = 9 * C
KPAD = 96
STEPS = CHUNKS * HEADS
LEAD = 3

PE_ORDER = """
    S0:0 T21:2 T22:2 S1:0 T23:2 M4:2 S2:0 T24:2 S3:0 T25:2 M5:2 S4:0 S5:0 T0:1 M6:2 T1:1 S6:0 T2:1 S7:0
    T3:1 T4:1 T5:1 S8:0 S9:0 T6:1 T7:1 U0:2 M0:1 T8:1 S10:0 T9:1 T10:1 S11:0 T11:1 M1:1 S12:0 T12:1
    T13:1 T14:1 S13:0 M2:1 T15:1 T16:1 S14:0 T17:1 S15:0 T18:1 T19:1 M3:1 T20:1"""
DVE_ORDER = """
    E19:2 E20:2 R3:1 A0:0 A1:0 A2:0 A3:0 E24:2 A4:0 A5:0 A6:0 R0:0 A7:0 P0:2 E5:1 A8:0 R1:0 E6:1 A9:0
    A10:0 E9:1 A11:0 E11:1 E12:1 A12:0 R2:0 A13:0 A14:0 E18:1 A15:0"""
ACT_ORDER = """
    X2:1 E21:2 E22:2 E23:2 X3:1 E25:2 E0:1 E1:1 E2:1 E3:1 E4:1 X0:0 E7:1 O0:2 E8:1 E10:1 X1:0 E13:1
    E14:1 E15:1 E16:1 E17:1"""


def ordered(text):
    return [(word[0], int(word[1:].split(":")[0]), int(word.split(":")[1])) for word in text.split()]


def attention(nc, sem, adj, q_planes, k_planes, v_tiles, sums):
    with ExitStack() as ctx:
        def sb(name, shape, dt=fp32):
            return ctx.enter_context(nc.sbuf_tensor(name, shape, dt))

        def psum(name, shape):
            return ctx.enter_context(nc.psum_tensor(name, shape, fp32))

        NS = len(SUBS)
        UNITS = banks(N, 1024)
        NU = len(UNITS) * NS
        GROUPS = -(-RT // 4)
        RING = 8
        pe_order, dve_order, act_order = ordered(PE_ORDER), ordered(DVE_ORDER), ordered(ACT_ORDER)
        BY_DVE = [i for kind, i, _ in sorted(dve_order) if kind == "E"]
        BY_ACT = [i for kind, i, _ in sorted(act_order) if kind == "E"]
        assert sorted(BY_DVE + BY_ACT) == list(range(RT))
        turns = [(kind, i, lag) for kind, i, lag in pe_order if kind in "TU"]
        bank = {(kind, i): n % 3 for n, (kind, i, _) in enumerate(turns)}
        assert len(turns) == RT + 1 and len(turns) % 3 == 0

        k_op = [sb(f"a_k{i}", [KPAD, N], bf16) for i in range(2)]
        q_op = [sb(f"a_q{i}", [KPAD, CHUNK], bf16) for i in range(2)]
        v_op = [sb(f"a_v{i}", [128, RT, C + 1]) for i in range(2)]
        adj_rows = sb("a_adj", [120, NS, N])
        probs = [sb(f"a_probs{i}", [120, NS, N]) for i in range(2)]
        unit_max = sb("a_unit_max", [120, 2, NS, len(UNITS)])
        neg_max = sb("a_neg_max", [120, 2, NS])
        probs_t = sb("a_probs_t", [128, RING, CHUNK])
        partial = sb("a_partial", [128, 2, CHUNK])
        total = sb("a_total", [C + 1, 2, CHUNK])
        ident = sb("a_ident", [128, 128])
        select = sb("a_select", [128, C + 1])
        score = [psum(f"a_score{i}", [128, 1024]) for i in range(2)]
        turn = psum("a_turn", [128, 3, 512])
        acc = psum("a_acc", [128, 512])

        ident_made, select_made = sem("a_ident_made"), sem("a_select_made")
        adj_loaded = sem("a_adj_loaded")
        qk_loaded = [sem(f"a_qk_loaded{i}") for i in range(2)]
        v_loaded = [sem(f"a_v_loaded{i}") for i in range(2)]
        scored = sem("a_scored")
        unit_done = sem("a_unit_done")
        max_ready = sem("a_max_ready")
        probs_ready = sem("a_probs_ready")
        turned = sem("a_turned")
        emptied_dve, emptied_act = sem("a_emptied_dve"), sem("a_emptied_act")
        multiplied = sem("a_multiplied")
        acc_zeroed = sem("a_acc_zeroed")
        acc_taken = sem("a_acc_taken")
        summed = sem("a_summed")
        total_ready = sem("a_total_ready")
        total_zeroed = sem("a_total_zeroed")
        stored = [sem(f"a_stored{i}") for i in range(2)]
        padded = sem("a_padded")
        passed_dve, passed_sp = sem("a_passed_dve"), sem("a_passed_sp")

        def units_scored(t, u):
            return t * NU + (2 * NU + u)

        def groups_multiplied(h, g):
            return h * GROUPS + (2 * GROUPS + g)

        def plan(order, t, p):
            for kind, i, lag in order:
                if not isinstance(t, int) or 0 <= t - lag < STEPS:
                    yield kind, i, t - lag, (p - lag) % 2

        def emptied(eng, head, v):
            if v in BY_DVE:
                eng.wait_ge(emptied_dve, len(BY_DVE) * head + sum(w <= v for w in BY_DVE))
            else:
                eng.wait_ge(emptied_act, len(BY_ACT) * head + sum(w <= v for w in BY_ACT))

        def steps(eng, body):
            for t in range(2):
                body(t, t % 2)
            with eng.Fori(1, STEPS // 2) as pair:
                for p in range(2):
                    body(pair * 2 + p, p)
            for t in range(STEPS, STEPS + 2):
                body(t, t % 2)

        block = ctx.enter_context(nc.Block())

        @block.sync
        def _(sp):
            sp.wait_ge(padded, 4)
            with sp.Fori(0, CHUNKS) as chunk:
                sp.wait_ge(adj_loaded, chunk * (16 * NS) + 16 * NS)
                sp.sem_inc(passed_sp, 1)
                with sp.Fori(0, HEADS // 2) as pair:
                    for p in range(2):
                        head = pair * 2 + p
                        step = chunk * HEADS + head
                        sp.wait_ge(scored, units_scored(step - 1, 0))
                        for s in range(3):
                            for r in range(3):
                                at = s * 3 * C + r * C
                                sp.dma_start(k_op[p][at:at + C, :], k_planes[s, :, bass.ds(head * N, N)]) \
                                    .then_inc(qk_loaded[p], 16)
                            sp.dma_start(q_op[p][s * 3 * C:(s + 1) * 3 * C, :],
                                         q_planes.rearrange("s c n -> (s c) n")
                                         [:, bass.ds(head * N + chunk * CSTEP, CHUNK)]) \
                                .then_inc(qk_loaded[p], 16)
                        sp.wait_ge(total_ready, step + 1)
                        if p == 0:
                            sp.wait_ge(total_zeroed, 1)
                        sp.dma_start(sums[bass.ds(step, 1)].rearrange("o c n -> (o c) n"),
                                     total[:, (p - LEAD) % 2, :]).then_inc(stored[p], 16)
            for i in range(LEAD):
                sp.wait_ge(total_ready, STEPS + i + 1)
                sp.dma_start(sums[STEPS + i], total[:, (STEPS + i - LEAD) % 2, :]) \
                    .then_inc(stored[(STEPS + i) % 2], 16)
            for i in range(2):
                sp.wait_ge(stored[i], 16 * len(range(i, STEPS + LEAD, 2)))

        @block.gpsimd
        def _(pool):
            write_identity(nc, pool, ident, ident_made)
            pool.memset(select[:, :], 0.0).then_inc(select_made, 1)
            for j in range(4):
                pool.wait_ge(select_made, j + 1)
                pool.affine_select(out=select[:, :], in_=select[:, :], compare_op=ALU.not_equal, fill=1.0,
                                   base=-32 * j, pattern=[[-1, C + 1]], channel_multiplier=1) \
                    .then_inc(select_made, 1)

            def load_adj(chunk, first=False):
                for s, (a, w) in enumerate(SUBS):
                    if not first:
                        pool.wait_ge(unit_done, chunk * (HEADS * NU) - (NU - NU // NS * (s + 1)))
                    pool.dma_start(adj_rows[0:w, s, :], adj[bass.ds(chunk * CSTEP + a, w)]) \
                        .then_inc(adj_loaded, 16)

            def load_values(chunk):
                with pool.Fori(0, HEADS // 2) as pair:
                    for p in range(2):
                        head = pair * 2 + p
                        pool.wait_ge(multiplied, groups_multiplied(chunk * HEADS + head - 1, 0))
                        pool.dma_start(v_op[p][:, :, :].rearrange("p t c -> p (t c)"),
                                       v_tiles[bass.ds(head, 1)].rearrange("o p n -> (o p) n")) \
                            .then_inc(v_loaded[p], 16)

            load_adj(0, first=True)
            with pool.Fori(0, CHUNKS - 1) as chunk:
                load_values(chunk)
                load_adj(chunk + 1)
            load_values(CHUNKS - 1)

        @block.tensor
        def _(pe):
            pe.sem_inc(scored, 2 * NU)
            pe.sem_inc(multiplied, 2 * GROUPS)
            pe.sem_inc(summed, 2)
            pe.wait_ge(ident_made, 2)
            pe.wait_ge(select_made, 5)

            def score_unit(t, p, u):
                s, j = divmod(u, len(UNITS))
                w, (m0, mw) = SUBS[s][1], UNITS[j]
                if u == 0:
                    pe.wait_ge(qk_loaded[p], 16 * 12 * (t // 2 + 1) if isinstance(t, int)
                               else (t - p) * 96 + 192)
                if not isinstance(t, int) or t * NU + u >= 2:
                    pe.wait_ge(unit_done, t * NU + u - 1)
                for a, n in banks(mw):
                    mm = pe.matmul(score[u % 2][0:w, a:a + n], q_op[p][:, SUBS[s][0]:SUBS[s][0] + w],
                                   k_op[p][:, m0 + a:m0 + a + n], start=True, stop=True)
                mm.then_inc(scored, 1)

            def turn_free(t, kind, i):
                n = [user[:2] for user in turns].index((kind, i))
                before, j, lag = turns[n - 3]
                head = t - lag - (1 if n < 3 else 0)
                if isinstance(t, int) and not 0 <= head < STEPS:
                    return
                if before == "T":
                    emptied(pe, head, j)
                else:
                    pe.wait_ge(total_ready, head + LEAD + 1)

            def turn_tile(t, h, p, v):
                if v == 0:
                    pe.wait_ge(probs_ready, h * NS + NS)
                turn_free(t, "T", v)
                n = width(v)
                for s, (a, w) in enumerate(SUBS):
                    mm = pe.transpose(turn[0:n, bank["T", v], a:a + w], probs[p][0:w, s, v * 128:v * 128 + n],
                                      ident[0:w, 0:w])
                mm.then_inc(turned, 1)

            def multiply(h, p, g):
                group = range(4 * g, min(4 * g + 4, RT))
                for owner in (BY_DVE, BY_ACT):
                    for v in [v for v in group if v in owner][-1:]:
                        emptied(pe, h, v)
                if g == 0:
                    pe.wait_ge(v_loaded[p], 16 * (h // 2 + 1) if isinstance(h, int) else (h - p) * 8 + 16)
                    pe.wait_ge(acc_zeroed, 1)
                    if not isinstance(h, int) or h > 0:
                        pe.wait_ge(acc_taken, h)
                for v in group:
                    n = width(v)
                    mm = pe.matmul(acc[32 * (v % 4):32 * (v % 4) + C + 1, 0:CHUNK], v_op[p][0:n, v, :],
                                   probs_t[0:n, v % RING, :], start=(v < 4), stop=(v >= RT - 4))
                mm.then_inc(multiplied, 1)

            def add_up(t, h, p):
                pe.wait_ge(acc_taken, h + 1)
                turn_free(t, "U", 0)
                pe.matmul(turn[0:C + 1, bank["U", 0], 0:CHUNK], select[:, :], partial[:, p, :],
                          start=True, stop=True).then_inc(summed, 1)

            def body(t, p):
                for kind, i, head, parity in plan(pe_order, t, p):
                    if kind == "S":
                        score_unit(head, parity, i)
                    elif kind == "T":
                        turn_tile(t, head, parity, i)
                    elif kind == "M":
                        multiply(head, parity, i)
                    else:
                        add_up(t, head, parity)

            steps(pe, body)

        def empty_tile(eng, h, v):
            n = width(v)
            eng.wait_ge(turned, h * RT + v + 1)
            if v >= RING:
                eng.wait_ge(multiplied, groups_multiplied(h, (v - RING) // 4 + 1))
            elif not isinstance(h, int) or h > 0:
                last = max(w for w in range(RT) if w % RING == v % RING)
                eng.wait_ge(multiplied, groups_multiplied(h - 1, last // 4 + 1))
            out, in_ = probs_t[0:n, v % RING, :], turn[0:n, bank["T", v], 0:CHUNK]
            if v in BY_DVE:
                eng.tensor_copy(out, in_).then_inc(emptied_dve, 1)
            else:
                eng.activation(out, in_, ACT.Copy).then_inc(emptied_act, 1)

        @block.vector
        def _(dve):
            dve.memset(acc[:, :], 0.0).then_inc(acc_zeroed, 1)
            for op in (*k_op, *q_op):
                dve.memset(op[64:KPAD, :], 0.0).then_inc(padded, 1)
            dve.memset(total[:, :, :].rearrange("c b n -> c (b n)"), 0.0).then_inc(total_zeroed, 1)
            dve.wait_ge(total_zeroed, 1)
            dve.sem_inc(total_ready, LEAD)

            def add_adj(t, p, u):
                s, j = divmod(u, len(UNITS))
                w, (m0, mw) = SUBS[s][1], UNITS[j]
                dve.wait_ge(scored, units_scored(t, u + 1))
                if s == 0 and after(t, 2):
                    dve.wait_ge(turned, t * RT - 2 * RT + min(RT, -(-(m0 + mw) // 128)))
                dve.sem_inc(passed_dve, 1)
                dve.tensor_tensor_reduce(out=probs[p][0:w, s, m0:m0 + mw], in0=score[u % 2][0:w, 0:mw],
                                         in1=adj_rows[0:w, s, m0:m0 + mw], scale=2.0, scalar=LOWEST,
                                         op0=ALU.add, op1=ALU.max, accum_out=unit_max[0:w, p, s, j:j + 1]) \
                    .then_inc(unit_done, 1)

            def greatest(t, p, s):
                w = SUBS[s][1]
                dve.wait_ge(unit_done, t * NU + (s + 1) * len(UNITS))
                dve.tensor_reduce(out=neg_max[0:w, p, s:s + 1], in_=unit_max[0:w, p, s, :], axis=AX.X,
                                  op=ALU.max, negate=True).then_inc(max_ready, 1)

            def take_partial(h, p):
                dve.wait_ge(multiplied, groups_multiplied(h, GROUPS))
                dve.wait_ge(summed, h + 1)
                dve.tensor_copy(partial[:, p, :], acc[:, 0:CHUNK]).then_inc(acc_taken, 1)

            def body(t, p):
                for kind, i, head, parity in plan(dve_order, t, p):
                    if kind == "A":
                        add_adj(head, parity, i)
                    elif kind == "R":
                        greatest(head, parity, i)
                    elif kind == "E":
                        empty_tile(dve, head, i)
                    else:
                        take_partial(head, parity)

            steps(dve, body)

        @block.scalar
        def _(act):
            def exponentials(h, p, s):
                w = SUBS[s][1]
                act.wait_ge(max_ready, h * NS + s + 1)
                act.activation(probs[p][0:w, s, :], probs[p][0:w, s, :], ACT.Exp,
                               bias=neg_max[0:w, p, s:s + 1]).then_inc(probs_ready, 1)

            def take_total(h, p):
                act.wait_ge(summed, h + 3)
                act.wait_ge(stored[1 - p], h * 8 + 8 * p + 16)
                act.wait_ge(total_zeroed, 1)
                act.activation(total[:, p, :], turn[0:C + 1, bank["U", 0], 0:CHUNK], ACT.Copy) \
                    .then_inc(total_ready, 1)

            def body(t, p):
                for kind, i, head, parity in plan(act_order, t, p):
                    if kind == "X":
                        exponentials(head, parity, i)
                    elif kind == "E":
                        empty_tile(act, head, i)
                    else:
                        take_total(head, parity)

            steps(act, body)


def gather_sums(nc, sem, sums, sum_planes):
    stored = sem("g_stored")
    per_head = sum_planes.rearrange("c (h n) -> c h n", n=N)
    with nc.Block() as block:
        @block.sync
        def _(sp):
            with sp.Fori(0, CHUNKS - 1) as chunk:
                for c in range(C + 1):
                    sp.dma_start(per_head[c, :, bass.ds(chunk * CSTEP, CSTEP)],
                                 sums[bass.ds(chunk * HEADS + LEAD, HEADS), c, 0:CSTEP]).then_inc(stored, 16)
            for c in range(C + 1):
                sp.dma_start(per_head[c, :, (CHUNKS - 1) * CSTEP:N],
                             sums[(CHUNKS - 1) * HEADS + LEAD:STEPS + LEAD, c, :]).then_inc(stored, 16)
            sp.wait_ge(stored, 16 * (C + 1) * CHUNKS)


def join_heads(nc, sem, x, sum_planes, Wo, x_rows, y_rows):
    with ExitStack() as ctx:
        def sb(name, shape, dt=fp32):
            return ctx.enter_context(nc.sbuf_tensor(name, shape, dt))

        planes = sb("j_planes", [128, 2, C + 1, 128])
        inverse = sb("j_inverse", [128, 2, 128])
        heads = sb("j_heads", [128, 2, C, 128])
        heads_t = sb("j_heads_t", [128, 2, C, 128])
        wo_in = sb("j_wo_in", [128, FEAT])
        wo_t = sb("j_wo_t", [128, C, D])
        ident = sb("j_ident", [128, 128])
        turn = ctx.enter_context(nc.psum_tensor("j_turn", [128, 2, 2, 512], fp32))
        joined = ctx.enter_context(nc.psum_tensor("j_joined", [128, 2, 512], fp32))
        ident_made, x_loaded, wo_loaded = sem("j_ident_made"), sem("j_x_loaded"), sem("j_wo_loaded")
        y_zeroed, wo_turned, wo_copied = sem("j_y_zeroed"), sem("j_wo_turned"), sem("j_wo_copied")
        loaded = [sem(f"j_loaded{i}") for i in range(2)]
        inverted, scaled, turned = sem("j_inverted"), sem("j_scaled"), sem("j_turned")
        copied, multiplied, added = sem("j_copied"), sem("j_multiplied"), sem("j_added")
        block = ctx.enter_context(nc.Block())

        @block.sync
        def _(sp):
            sp.dma_start(wo_in[:, :], Wo).then_inc(wo_loaded, 16)
            sp.wait_ge(y_zeroed, 2)
            sp.dma_start(x_rows[:, 0:RT - 1, :], x[0:128 * (RT - 1)].rearrange("(t p) d -> p t d", p=128)) \
                .then_inc(x_loaded, 16)
            sp.dma_start(x_rows[0:LAST, RT - 1, :], x[128 * (RT - 1):N]).then_inc(x_loaded, 16)

            def body(t, p):
                if after(t, 2):
                    sp.wait_ge(scaled, t - 1)
                sp.dma_start(planes[0:width(t), p], sum_planes[:, bass.ds(t * (128 * 128), width(t) * 128)]
                             .rearrange("c (r j) -> r c j", j=128)).then_inc(loaded[p], 16)

            tiles(sp, body)

        @block.gpsimd
        def _(pool):
            write_identity(nc, pool, ident, ident_made)

        @block.tensor
        def _(pe):
            pe.wait_ge(ident_made, 2)
            pe.wait_ge(wo_loaded, 16)
            for c in range(C):
                mm = pe.transpose(turn[:, 0, c // 4, c % 4 * 128:c % 4 * 128 + 128], wo_in[:, c:FEAT:C],
                                  ident[:, :])
            mm.then_inc(wo_turned, 1)
            pe.wait_ge(wo_copied, 1)

            def body(t, p):
                n = width(t)
                pe.wait_ge(scaled, t + 1)
                if after(t, 2):
                    pe.wait_ge(copied, t - 1)
                for c in range(C):
                    mm = pe.transpose(turn[:, p, c // 4, c % 4 * 128:c % 4 * 128 + n], heads[0:n, p, c],
                                      ident[0:n, 0:n])
                mm.then_inc(turned, 1)
                pe.wait_ge(copied, t + 1)
                if after(t, 2):
                    pe.wait_ge(added, t - 1)
                for c in range(C):
                    mm = pe.matmul(joined[0:n, p, 0:D], heads_t[:, p, c, 0:n], wo_t[:, c, :],
                                   start=(c == 0), stop=(c == C - 1))
                mm.then_inc(multiplied, 1)

            tiles(pe, body)

        @block.scalar
        def _(act):
            def body(t, p):
                n = width(t)
                act.wait_ge(turned, t + 1)
                if after(t, 2):
                    act.wait_ge(multiplied, t - 1)
                act.activation(heads_t[:, p, :, 0:n],
                               turn[:, p].rearrange("j b (c r) -> j (b c) r", c=4)[:, :, 0:n], ACT.Copy) \
                    .then_inc(copied, 1)

            tiles(act, body)

        @block.vector
        def _(dve):
            dve.memset(x_rows[:, :, :].rearrange("p t d -> p (t d)"), 0.0).then_inc(y_zeroed, 1)
            dve.memset(y_rows[:, :, :].rearrange("p t d -> p (t d)"), 0.0).then_inc(y_zeroed, 1)
            dve.wait_ge(wo_turned, 1)
            dve.tensor_copy(wo_t[:, :, :].rearrange("j c e -> j (c e)"),
                            turn[:, 0].rearrange("j b n -> j (b n)")).then_inc(wo_copied, 1)
            dve.wait_ge(x_loaded, 32)

            def add(t, p):
                dve.wait_ge(multiplied, t + 1)
                dve.tensor_tensor(row_of(y_rows, t), joined[0:width(t), p, 0:D], row_of(x_rows, t), ALU.add) \
                    .then_inc(added, 1)

            def body(t, p):
                n = width(t)
                dve.wait_ge(loaded[p], count(t, p))
                dve.reciprocal(inverse[0:n, p], planes[0:n, p, C]).then_inc(inverted, 1)
                if after(t, 2):
                    dve.wait_ge(turned, t - 1)
                dve.wait_ge(inverted, t + 1)
                dve.tensor_tensor(heads[0:n, p], planes[0:n, p, 0:C],
                                  inverse[0:n, p].unsqueeze(1).broadcast_to([n, C, 128]), ALU.mult) \
                    .then_inc(scaled, 1)
                if after(t, 1):
                    add(t - 1, 1 - p)

            tiles(dve, body)
            add(RT - 1, 1)


def layer_norm(nc, sem, tag, y_rows, x_rows):
    with ExitStack() as ctx:
        total = ctx.enter_context(nc.sbuf_tensor(f"{tag}_total", [128, RT], fp32))
        scale = ctx.enter_context(nc.sbuf_tensor(f"{tag}_scale", [128, RT], fp32))
        stepped, rooted = sem(f"{tag}_stepped"), sem(f"{tag}_rooted")
        block = ctx.enter_context(nc.Block())

        def spread(small):
            return small[:, :].unsqueeze(2).broadcast_to([128, RT, D])

        @block.scalar
        def _(act):
            act.wait_ge(stepped, 6)
            act.activation(scale[:, :], total[:, :], ACT.Sqrt).then_inc(rooted, 1)

        @block.vector
        def _(dve):
            x, y = x_rows[:, :, :], y_rows[:, :, :]
            steps = [
                lambda: dve.tensor_reduce(out=total[:, :], in_=y, axis=AX.X, op=ALU.add),
                lambda: dve.tensor_scalar(total[:, :], total[:, :], 1.0 / D, None, ALU.mult),
                lambda: dve.tensor_tensor(y, y, spread(total), ALU.subtract),
                lambda: dve.tensor_tensor(x, y, y, ALU.mult),
                lambda: dve.tensor_reduce(out=total[:, :], in_=x, axis=AX.X, op=ALU.add),
                lambda: dve.tensor_scalar(total[:, :], total[:, :], 1.0 / D, 1e-5, ALU.mult, ALU.add),
                lambda: dve.reciprocal(scale[:, :], scale[:, :]),
                lambda: dve.tensor_tensor(x, y, spread(scale), ALU.mult),
            ]
            for i, step in enumerate(steps):
                if i == 6:
                    dve.wait_ge(rooted, 1)
                step().then_inc(stepped, 1)
                dve.wait_ge(stepped, i + 1)


class Gram:
    def __init__(self, nc, ctx, tag):
        self.xt = ctx.enter_context(nc.sbuf_tensor(f"{tag}_xt", [128, N], fp32))
        self.square_along = ctx.enter_context(nc.sbuf_tensor(f"{tag}_square_along", [128, N], fp32))
        self.square = ctx.enter_context(nc.sbuf_tensor(f"{tag}_square", [128, RT], fp32))


def prepare_gram(nc, sem, tag, rows, gram, root):
    with ExitStack() as ctx:
        ident = ctx.enter_context(nc.sbuf_tensor(f"{tag}g_ident", [128, 128], fp32))
        ones = ctx.enter_context(nc.sbuf_tensor(f"{tag}g_ones", [128, 128], fp32))
        xt2 = ctx.enter_context(nc.sbuf_tensor(f"{tag}g_xt2", [128, N], fp32))
        rows2 = ctx.enter_context(nc.sbuf_tensor(f"{tag}g_rows2", [128, RT, D], fp32))
        turn = ctx.enter_context(nc.psum_tensor(f"{tag}g_turn", [128, 4, 512], fp32))
        spread = ctx.enter_context(nc.psum_tensor(f"{tag}g_spread", [128, 4, 512], fp32))
        ident_made, ones_made, turned = sem(f"{tag}g_ident_made"), sem(f"{tag}g_ones_made"), sem(f"{tag}g_turned")
        copied, squared, spread_done = sem(f"{tag}g_copied"), sem(f"{tag}g_squared"), sem(f"{tag}g_spread_done")
        taken, summed = sem(f"{tag}g_taken"), sem(f"{tag}g_summed")
        pieces = banks(N)
        block = ctx.enter_context(nc.Block())

        @block.gpsimd
        def _(pool):
            write_identity(nc, pool, ident, ident_made)
            pool.memset(ones[:, :], 1.0).then_inc(ones_made, 1)

        @block.tensor
        def _(pe):
            pe.wait_ge(ident_made, 2)
            for b, (a, n) in enumerate(pieces):
                if b >= 4:
                    pe.wait_ge(copied, b - 3)
                for t in range(4 * b, min(4 * b + 4, RT)):
                    w = width(t)
                    mm = pe.transpose(turn[:, b % 4, t % 4 * 128:t % 4 * 128 + w], rows[0:w, t, :],
                                      ident[0:w, 0:w])
                mm.then_inc(turned, 1)
            pe.wait_ge(ones_made, 1)
            for b, (a, n) in enumerate(pieces):
                pe.wait_ge(squared, b + 1)
                if b >= 4:
                    pe.wait_ge(taken, b - 3)
                pe.matmul(spread[:, b % 4, 0:n], ones[:, :], xt2[:, a:a + n], start=True, stop=True) \
                    .then_inc(spread_done, 1)

        @block.vector
        def _(dve):
            for b, (a, n) in enumerate(pieces):
                dve.wait_ge(turned, b + 1)
                dve.tensor_copy(gram.xt[:, a:a + n], turn[:, b % 4, 0:n]).then_inc(copied, 1)
                dve.wait_ge(copied, b + 1)
                dve.tensor_tensor(xt2[:, a:a + n], gram.xt[:, a:a + n], gram.xt[:, a:a + n], ALU.mult) \
                    .then_inc(squared, 1)
            dve.tensor_tensor(rows2[:, :, :], rows[:, :, :], rows[:, :, :], ALU.mult).then_inc(summed, 1)
            dve.wait_ge(summed, 1)
            dve.tensor_reduce(out=gram.square[:, :], in_=rows2[:, :, :], axis=AX.X, op=ALU.add) \
                .then_inc(summed, 1)

        @block.scalar
        def _(act):
            func = ACT.Sqrt if root else ACT.Copy
            for b, (a, n) in enumerate(pieces):
                act.wait_ge(spread_done, b + 1)
                act.activation(gram.square_along[:, a:a + n], spread[:, b % 4, 0:n], func).then_inc(taken, 1)
            if root:
                act.wait_ge(summed, 2)
                act.activation(gram.square[:, :], gram.square[:, :], func).then_inc(taken, 1)


def column_of(buffer, t):
    return buffer[0:width(t), t:t + 1] if isinstance(t, int) else buffer[:, bass.ds(t, 1)]


def ring_free(t, i):
    return t * 7 + (i - 2 if i else 0)


def tile_groups():
    return [[(k, (k - 4 * g) * 128, width(k)) for k in range(4 * g, min(4 * g + 4, RT))]
            for g in range(-(-RT // 4))]


def cosine_attention(nc, sem, adj, beta, gram, x_rows, y_rows):
    pieces, groups = banks(N), tile_groups()
    NP, NG = len(pieces), len(groups)
    with ExitStack() as ctx:
        def sb(name, shape, dt=fp32):
            return ctx.enter_context(nc.sbuf_tensor(name, shape, dt))

        mask = sb("c_mask", [128, 2, N])
        product = sb("c_product", [128, N])
        score = sb("c_score", [128, 2, N])
        own_t = sb("c_own_t", [128, 2, 128])
        own_norm = sb("c_own_norm", [128, 2, 1])
        peak, neg_peak = sb("c_peak", [128, 2, 1]), sb("c_neg_peak", [128, 2, 1])
        weight, inverse = sb("c_weight", [128, 2, 1]), sb("c_inverse", [128, 2, 1])
        score_t = sb("c_score_t", [128, 3, 512])
        beta_in, beta_all = sb("c_beta_in", [1, 1]), sb("c_beta_all", [128, 1])
        ones, ident = sb("c_ones", [1, 128]), sb("c_ident", [128, 128])
        dots = ctx.enter_context(nc.psum_tensor("c_dots", [128, 3, 512], fp32))
        turn = ctx.enter_context(nc.psum_tensor("c_turn", [128, 3, 512], fp32))
        out = ctx.enter_context(nc.psum_tensor("c_out", [128, 2, 512], fp32))
        ident_made, beta_loaded, beta_spread = sem("c_ident_made"), sem("c_beta_loaded"), sem("c_beta_spread")
        zeroed, loaded = sem("c_zeroed"), [sem(f"c_loaded{i}") for i in range(2)]
        own_ready, norm_ready, masked = sem("c_own_ready"), sem("c_norm_ready"), sem("c_masked")
        dotted, divided, steps = sem("c_dotted"), sem("c_divided"), sem("c_steps")
        inverted = sem("c_inverted")
        probs_ready, turned, emptied = sem("c_probs_ready"), sem("c_turned"), sem("c_emptied")
        multiplied, finished = sem("c_multiplied"), sem("c_finished")
        passed_dve, passed_pool = sem("c_passed_dve"), sem("c_passed_pool")
        DS = 4
        block = ctx.enter_context(nc.Block())

        @block.sync
        def _(sp):
            sp.dma_start(beta_in[:, :], beta.rearrange("(a n) -> a n", a=1)).then_inc(beta_loaded, 16)

            def body(t, p):
                if after(t, 2):
                    sp.wait_ge(steps, t * DS - (DS + 1))
                sp.dma_start(mask[0:width(t), p, :], adj[node_rows(t)]).then_inc(loaded[p], 16)

            tiles(sp, body)

        @block.gpsimd
        def _(pool):
            write_identity(nc, pool, ident, ident_made)
            pool.memset(ones[:, :], 1.0).then_inc(ident_made, 1)

            def body(t, p):
                if after(t, 2):
                    pool.wait_ge(dotted, t * NP - NP)
                    pool.sem_inc(passed_pool, 1)
                pool.tensor_copy(own_t[:, p, 0:width(t)], gram.xt[:, node_rows(t)]).then_inc(own_ready, 1)

            tiles(pool, body)

        @block.tensor
        def _(pe):
            pe.wait_ge(ident_made, 3)
            pe.wait_ge(beta_loaded, 16)
            pe.wait_ge(zeroed, 1)
            pe.matmul(out[:, 0, 0:1], ones[:, :], beta_in[:, :], start=True, stop=True).then_inc(beta_spread, 1)
            pe.wait_ge(beta_spread, 2)

            def dot(t, p):
                pe.wait_ge(own_ready, t + 1)
                for b, (a, w) in enumerate(pieces):
                    if after(t, 1) or b >= 3:
                        pe.wait_ge(divided, ring_free(t, b))
                    pe.matmul(dots[0:width(t), b % 3, 0:w], own_t[:, p, 0:width(t)], gram.xt[:, a:a + w],
                              start=True, stop=True).then_inc(dotted, 1)

            def aggregate(t, p):
                n = width(t)
                pe.wait_ge(probs_ready, t + 1)
                for g in range(NG + 1):
                    if g < NG:
                        if after(t, 1) or g >= 3:
                            pe.wait_ge(emptied, ring_free(t, g))
                        for k, a, w in groups[g]:
                            mm = pe.transpose(turn[0:w, g % 3, a:a + n],
                                              score[0:n, p, k * 128:k * 128 + w], ident[0:n, 0:n])
                        mm.then_inc(turned, 1)
                    if g >= 1:
                        pe.wait_ge(emptied, t * NG + g)
                        if g == 1 and after(t, 2):
                            pe.wait_ge(finished, t - 1)
                        for k, a, w in groups[g - 1]:
                            mm = pe.matmul(out[0:n, p, 0:D], score_t[0:w, (g - 1) % 3, a:a + n],
                                           x_rows[0:w, k, :], start=(k == 0), stop=(k == RT - 1))
                        mm.then_inc(multiplied, 1)

            def body(t, p):
                if not isinstance(t, int) or t < RT:
                    dot(t, p)
                if after(t, 1):
                    aggregate(t - 1, 1 - p)

            tiles(pe, body, end=RT + 1)

        @block.vector
        def _(dve):
            dve.memset(turn[:, :, :].rearrange("p b n -> p (b n)"), 0.0).then_inc(zeroed, 1)
            dve.wait_ge(beta_spread, 1)
            dve.tensor_copy(beta_all[:, :], out[:, 0, 0:1]).then_inc(beta_spread, 1)
            dve.wait_ge(beta_spread, 2)

            def scores(t, p):
                n, base = width(t), t * DS
                dve.tensor_copy(own_norm[0:n, p], column_of(gram.square, t)).then_inc(norm_ready, 1)
                dve.wait_ge(norm_ready, t + 1)
                dve.tensor_scalar(product[0:n], gram.square_along[0:n], own_norm[0:n, p], 1e-7,
                                  ALU.mult, ALU.add).then_inc(steps, 1)
                dve.wait_ge(steps, base + 1)
                dve.reciprocal(product[0:n], product[0:n]).then_inc(steps, 1)
                dve.wait_ge(steps, base + 2)
                if after(t, 2):
                    dve.wait_ge(turned, t * NG - NG)
                for b, (a, w) in enumerate(pieces):
                    dve.wait_ge(dotted, t * NP + (b + 1))
                    dve.scalar_tensor_tensor(out=score[0:n, p, a:a + w], in0=dots[0:n, b % 3, 0:w],
                                             scalar=beta_all[0:n], in1=product[0:n, a:a + w],
                                             op0=ALU.mult, op1=ALU.mult).then_inc(divided, 1)
                dve.wait_ge(divided, t * NP + NP)
                dve.wait_ge(masked, t * 2 + 2)
                dve.sem_inc(passed_dve, 1)
                dve.tensor_tensor_reduce(out=score[0:n, p, :], in0=score[0:n, p, :], in1=mask[0:n, p, :],
                                         scale=1.0, scalar=LOWEST, op0=ALU.add, op1=ALU.max,
                                         accum_out=peak[0:n, p]).then_inc(steps, 1)
                dve.wait_ge(steps, base + 3)
                dve.tensor_scalar(neg_peak[0:n, p], peak[0:n, p], -1.0, None, ALU.mult).then_inc(steps, 1)

            def finish(t, p):
                n = width(t)
                dve.wait_ge(probs_ready, t + 1)
                dve.reciprocal(inverse[0:n, p], weight[0:n, p]).then_inc(inverted, 1)
                dve.wait_ge(multiplied, t * NG + NG)
                dve.wait_ge(inverted, t + 1)
                dve.scalar_tensor_tensor(out=row_of(y_rows, t), in0=out[0:n, p, 0:D], scalar=inverse[0:n, p],
                                         in1=row_of(x_rows, t), op0=ALU.mult, op1=ALU.add).then_inc(finished, 1)

            def body(t, p):
                if not isinstance(t, int) or t < RT:
                    scores(t, p)
                if after(t, 1):
                    finish(t - 1, 1 - p)

            tiles(dve, body, end=RT + 1)

        @block.scalar
        def _(act):
            def scores(t, p):
                n = width(t)
                act.wait_ge(loaded[p], count(t, p))
                act.activation(mask[0:n, p, :], mask[0:n, p, :], ACT.Copy, scale=-1.0, bias=1.0) \
                    .then_inc(masked, 1)
                act.wait_ge(masked, t * 2 + 1)
                act.activation(mask[0:n, p, :], mask[0:n, p, :], ACT.Copy, scale=-1.0e9).then_inc(masked, 1)

            def probs(t, p):
                n = width(t)
                act.wait_ge(steps, t * DS + DS)
                act.activation(score[0:n, p, :], score[0:n, p, :], ACT.Exp, bias=neg_peak[0:n, p],
                               accum_out=weight[0:n, p]).then_inc(probs_ready, 1)

            def empty(t):
                for g in range(NG):
                    act.wait_ge(turned, t * NG + (g + 1))
                    if after(t, 1) or g >= 3:
                        act.wait_ge(multiplied, ring_free(t, g))
                    w = 512 if g < NG - 1 else len(groups[g]) * 128
                    act.activation(score_t[:, g % 3, 0:w], turn[:, g % 3, 0:w], ACT.Copy).then_inc(emptied, 1)

            def body(t, p):
                if not isinstance(t, int) or t < RT:
                    scores(t, p)
                if after(t, 1):
                    probs(t - 1, 1 - p)
                    empty(t - 1)

            tiles(act, body, end=RT + 1)


def convolve(nc, sem, tag, matrix, values, W, bias, kind, out_rows, x_rows=None, scale=None, row_sums=None):
    groups = tile_groups()
    NG = len(groups)
    silu = kind in ("silu", "silu_x")
    with ExitStack() as ctx:
        def sb(name, shape, dt=fp32):
            return ctx.enter_context(nc.sbuf_tensor(name, shape, dt))

        rows_in = sb(f"{tag}_rows_in", [128, 2, N])
        matrix_t = sb(f"{tag}_matrix_t", [128, 3, 512])
        hop_t = sb(f"{tag}_hop_t", [128, 2, 128])
        z = sb(f"{tag}_z", [128, 2, D])
        gate = sb(f"{tag}_gate", [128, 2, D])
        own_scale = sb(f"{tag}_own_scale", [128, 2, 1])
        w_in, bias_in, bias_all = sb(f"{tag}_w_in", [128, D]), sb(f"{tag}_bias_in", [1, D]), sb(f"{tag}_bias_all", [128, D])
        ones, ident = sb(f"{tag}_ones", [1, 128]), sb(f"{tag}_ident", [128, 128])
        turn = ctx.enter_context(nc.psum_tensor(f"{tag}_turn", [128, 3, 512], fp32))
        hop = ctx.enter_context(nc.psum_tensor(f"{tag}_hop", [128, 2, 512], fp32))
        mixed = ctx.enter_context(nc.psum_tensor(f"{tag}_mixed", [128, 2, 512], fp32))
        ident_made, w_loaded, bias_spread = sem(f"{tag}_ident_made"), sem(f"{tag}_w_loaded"), sem(f"{tag}_bias_spread")
        loaded = [sem(f"{tag}_loaded{i}") for i in range(2)]
        zeroed, turned, emptied = sem(f"{tag}_zeroed"), sem(f"{tag}_turned"), sem(f"{tag}_emptied")
        multiplied, hop_taken, mixed_done = sem(f"{tag}_multiplied"), sem(f"{tag}_hop_taken"), sem(f"{tag}_mixed_done")
        z_ready, gated, finished = sem(f"{tag}_z_ready"), sem(f"{tag}_gated"), sem(f"{tag}_finished")
        scale_taken, summed, silu_done = sem(f"{tag}_scale_taken"), sem(f"{tag}_summed"), sem(f"{tag}_silu_done")
        passed_sp = sem(f"{tag}_passed_sp")
        block = ctx.enter_context(nc.Block())

        @block.sync
        def _(sp):
            sp.dma_start(w_in[:, :], W).then_inc(w_loaded, 16)
            sp.dma_start(bias_in[:, :], bias.rearrange("(a n) -> a n", a=1)).then_inc(w_loaded, 16)

            def body(t, p):
                if after(t, 2):
                    sp.wait_ge(turned, t * NG - NG)
                    sp.sem_inc(passed_sp, 1)
                    if row_sums is not None:
                        sp.wait_ge(summed, t - 1)
                    sp.sem_inc(passed_sp, 1)
                sp.dma_start(rows_in[0:width(t), p, :], matrix[node_rows(t)]).then_inc(loaded[p], 16)

            tiles(sp, body)

        @block.gpsimd
        def _(pool):
            write_identity(nc, pool, ident, ident_made)
            pool.memset(ones[:, :], 1.0).then_inc(ident_made, 1)

        @block.tensor
        def _(pe):
            pe.wait_ge(ident_made, 3)
            pe.wait_ge(w_loaded, 32)
            pe.wait_ge(zeroed, 1)
            pe.matmul(mixed[:, 0, 0:D], ones[:, :], bias_in[:, :], start=True, stop=True).then_inc(bias_spread, 1)
            pe.wait_ge(bias_spread, 2)

            def mix(t, p):
                pe.wait_ge(hop_taken, t + 1)
                if after(t, 2):
                    pe.wait_ge(z_ready, t - 1)
                pe.matmul(mixed[0:width(t), p, 0:D], hop_t[:, p, 0:width(t)], w_in[:, :],
                          start=True, stop=True).then_inc(mixed_done, 1)

            def body(t, p):
                if isinstance(t, int) and t == RT:
                    mix(t - 1, 1 - p)
                    return
                n = width(t)
                pe.wait_ge(loaded[p], count(t, p))
                for g in range(NG + 1):
                    if g < NG:
                        if after(t, 1) or g >= 3:
                            pe.wait_ge(emptied, ring_free(t, g))
                        for k, a, w in groups[g]:
                            mm = pe.transpose(turn[0:w, g % 3, a:a + n], rows_in[0:n, p, k * 128:k * 128 + w],
                                              ident[0:n, 0:n])
                        mm.then_inc(turned, 1)
                    if g >= 1:
                        pe.wait_ge(emptied, t * NG + g)
                        if g == 1 and after(t, 2):
                            pe.wait_ge(hop_taken, t - 1)
                        for k, a, w in groups[g - 1]:
                            mm = pe.matmul(hop[:, p, 0:n], values[0:w, k, :],
                                           matrix_t[0:w, (g - 1) % 3, a:a + n],
                                           start=(k == 0), stop=(k == RT - 1))
                        mm.then_inc(multiplied, 1)
                    if g == 2 and after(t, 1):
                        mix(t - 1, 1 - p)

            tiles(pe, body, end=RT + 1)

        @block.scalar
        def _(act):
            def gate_tile(t, p):
                act.wait_ge(z_ready, t + 1)
                if after(t, 2):
                    act.wait_ge(finished, t - 1)
                act.activation(gate[0:width(t), p, :], z[0:width(t), p, :], ACT.Sigmoid).then_inc(gated, 1)

            def body(t, p):
                if isinstance(t, int) and t == RT:
                    if silu:
                        gate_tile(t - 1, 1 - p)
                    return
                for g in range(NG):
                    act.wait_ge(turned, t * NG + (g + 1))
                    if after(t, 1) or g >= 3:
                        act.wait_ge(multiplied, ring_free(t, g))
                    w = len(groups[g]) * 128
                    act.activation(matrix_t[:, g % 3, 0:w], turn[:, g % 3, 0:w], ACT.Copy).then_inc(emptied, 1)
                    if g == 4 and silu and after(t, 1):
                        gate_tile(t - 1, 1 - p)

            tiles(act, body, end=RT + 1)

        @block.vector
        def _(dve):
            dve.memset(turn[:, :, :].rearrange("p b n -> p (b n)"), 0.0).then_inc(zeroed, 1)
            dve.wait_ge(bias_spread, 1)
            dve.tensor_copy(bias_all[:, :], mixed[:, 0, 0:D]).then_inc(bias_spread, 1)
            dve.wait_ge(bias_spread, 2)

            def finish(t, p):
                n = width(t)
                if scale is not None:
                    dve.tensor_copy(own_scale[0:n, p], column_of(scale, t)).then_inc(scale_taken, 1)
                    dve.wait_ge(scale_taken, t + 1)
                dve.wait_ge(mixed_done, t + 1)
                if silu:
                    dve.tensor_tensor(z[0:n, p, :], mixed[0:n, p, 0:D], bias_all[0:n, :], ALU.add) \
                        .then_inc(z_ready, 1)
                    dve.wait_ge(gated, t + 1)
                    if kind == "silu":
                        dve.tensor_tensor(row_of(out_rows, t), z[0:n, p, :], gate[0:n, p, :], ALU.mult) \
                            .then_inc(finished, 1)
                        return
                    dve.tensor_tensor(z[0:n, p, :], z[0:n, p, :], gate[0:n, p, :], ALU.mult) \
                        .then_inc(silu_done, 1)
                    dve.wait_ge(silu_done, t + 1)
                else:
                    dve.scalar_tensor_tensor(out=z[0:n, p, :], in0=mixed[0:n, p, 0:D], scalar=own_scale[0:n, p],
                                             in1=bias_all[0:n, :], op0=ALU.mult, op1=ALU.add) \
                        .then_inc(z_ready, 1)
                    dve.wait_ge(z_ready, t + 1)
                if kind == "leaky":
                    dve.scalar_tensor_tensor(out=row_of(out_rows, t), in0=z[0:n, p, :], scalar=0.1,
                                             in1=z[0:n, p, :], op0=ALU.mult, op1=ALU.max).then_inc(finished, 1)
                else:
                    dve.tensor_tensor(row_of(out_rows, t), z[0:n, p, :], row_of(x_rows, t), ALU.add) \
                        .then_inc(finished, 1)

            def body(t, p):
                if isinstance(t, int) and t == RT:
                    finish(t - 1, 1 - p)
                    return
                n = width(t)
                if row_sums is not None:
                    dve.wait_ge(loaded[p], count(t, p))
                    dve.tensor_reduce(out=column_of(row_sums, t), in_=rows_in[0:n, p, :], axis=AX.X,
                                      op=ALU.add).then_inc(summed, 1)
                if after(t, 1):
                    finish(t - 1, 1 - p)
                dve.wait_ge(multiplied, t * NG + NG)
                if after(t, 2):
                    dve.wait_ge(mixed_done, t - 1)
                dve.tensor_copy(hop_t[:, p, 0:n], hop[:, p, 0:n]).then_inc(hop_taken, 1)

            tiles(dve, body, end=RT + 1)


def scale_rows(nc, sem, tag, row_sums, scale, x_rows, scaled):
    with nc.Block() as block:
        rooted, stepped = sem(f"{tag}_rooted"), sem(f"{tag}_stepped")

        @block.scalar
        def _(act):
            act.activation(scale[:, :], row_sums[:, :], ACT.Sqrt).then_inc(rooted, 1)

        @block.vector
        def _(dve):
            dve.wait_ge(rooted, 1)
            dve.reciprocal(scale[:, :], scale[:, :]).then_inc(stepped, 1)
            dve.wait_ge(stepped, 1)
            dve.tensor_tensor(scaled[:, :, :], x_rows[:, :, :],
                              scale[:, :].unsqueeze(2).broadcast_to([128, RT, D]), ALU.mult) \
                .then_inc(stepped, 1)


def nearest_neighbours(nc, sem, adj, gram, graph, row_sums):
    pieces = banks(N)
    NP = len(pieces)
    KEEP, TOP = 4, 8
    with ExitStack() as ctx:
        def sb(name, shape, dt=fp32):
            return ctx.enter_context(nc.sbuf_tensor(name, shape, dt))

        adj_in = sb("s_adj_in", [128, 2, N])
        squares = sb("s_squares", [128, 2, N])
        near = sb("s_near", [128, 2, N + TOP - KEEP])
        others = sb("s_others", [128, N + TOP - KEEP])
        top = sb("s_top", [128, 2, TOP])
        own_t = sb("s_own_t", [128, 2, 128])
        own_square = sb("s_own_square", [128, 2, 1])
        own_sum = sb("s_own_sum", [128, 2, 1])
        dots = ctx.enter_context(nc.psum_tensor("s_dots", [128, 6, 512], fp32))
        loaded = [sem(f"s_loaded{i}") for i in range(2)]
        stored = [sem(f"s_stored{i}") for i in range(2)]
        own_ready, square_ready, squares_ready = sem("s_own_ready"), sem("s_square_ready"), sem("s_squares_ready")
        dotted, subtracted, clamped = sem("s_dotted"), sem("s_subtracted"), sem("s_clamped")
        rooted, near_ready, stepped = sem("s_rooted"), sem("s_near_ready"), sem("s_stepped")
        ends_made, kept, graph_ready = sem("s_ends_made"), sem("s_kept"), sem("s_graph_ready")
        passed_dve, passed_pool = sem("s_passed_dve"), sem("s_passed_pool")
        block = ctx.enter_context(nc.Block())

        @block.sync
        def _(sp):
            def store(t, p):
                sp.wait_ge(graph_ready, t + 1)
                sp.dma_start(graph[node_rows(t)], adj_in[0:width(t), p, :]).then_inc(stored[p], 16)

            def body(t, p):
                if after(t, 2):
                    store(t - 2, p)
                    sp.wait_ge(stored[p], count(t - 2, p))
                sp.dma_start(adj_in[0:width(t), p, :], adj[node_rows(t)]).then_inc(loaded[p], 16)

            tiles(sp, body)
            for p in range(2):
                store(RT - 2 + p, p)
                sp.wait_ge(stored[p], 16 * RT // 2)

        @block.gpsimd
        def _(pool):
            def body(t, p):
                n = width(t)
                if after(t, 2):
                    pool.wait_ge(dotted, t * NP - NP)
                    pool.sem_inc(passed_pool, 1)
                pool.tensor_copy(own_t[:, p, 0:n], gram.xt[:, node_rows(t)]).then_inc(own_ready, 1)

            tiles(pool, body)

        @block.tensor
        def _(pe):
            def body(t, p):
                n = width(t)
                pe.wait_ge(own_ready, t + 1)
                for b, (a, w) in enumerate(pieces):
                    if b == 6:
                        pe.wait_ge(subtracted, t * NP + 1)
                    elif after(t, 1):
                        pe.wait_ge(subtracted, t * NP - (0 if b == 0 else NP - 1 - b))
                    pe.matmul(dots[0:n, b % 6, 0:w], own_t[:, p, 0:n], gram.xt[:, a:a + w],
                              start=True, stop=True).then_inc(dotted, 1)

            tiles(pe, body)

        @block.scalar
        def _(act):
            def body(t, p):
                n = width(t)
                act.wait_ge(square_ready, t + 1)
                if after(t, 2):
                    act.wait_ge(subtracted, t * NP - NP)
                act.activation(squares[0:n, p, :], gram.square_along[0:n, :], ACT.Identity,
                               bias=own_square[0:n, p]).then_inc(squares_ready, 1)
                act.wait_ge(clamped, t + 1)
                act.activation(near[0:n, p, 0:N], near[0:n, p, 0:N], ACT.Sqrt).then_inc(rooted, 1)
                act.wait_ge(rooted, t + 1)
                act.activation(near[0:n, p, 0:N], near[0:n, p, 0:N], ACT.Exp, scale=-0.5) \
                    .then_inc(near_ready, 1)

            tiles(act, body)

        @block.vector
        def _(dve):
            for p in range(2):
                dve.memset(near[:, p, N:], -1.0).then_inc(ends_made, 1)
            dve.wait_ge(ends_made, 2)

            def distances(t, p):
                n = width(t)
                dve.tensor_copy(own_square[0:n, p], column_of(gram.square, t)).then_inc(square_ready, 1)
                dve.wait_ge(squares_ready, t + 1)
                for b, (a, w) in enumerate(pieces):
                    dve.wait_ge(dotted, t * NP + (b + 1))
                    dve.scalar_tensor_tensor(out=near[0:n, p, a:a + w], in0=dots[0:n, b % 6, 0:w], scalar=-2.0,
                                             in1=squares[0:n, p, a:a + w], op0=ALU.mult, op1=ALU.add) \
                        .then_inc(subtracted, 1)
                dve.wait_ge(subtracted, t * NP + NP)
                dve.tensor_scalar(near[0:n, p, 0:N], near[0:n, p, 0:N], 0.0, 1e-10, ALU.max, ALU.add) \
                    .then_inc(clamped, 1)

            def keep(t, p):
                n, base = width(t), t * 5
                dve.wait_ge(near_ready, t + 1)
                dve.sem_inc(passed_dve, 1)
                dve.max(top[0:n, p, :], near[0:n, p, 0:N]).then_inc(stepped, 1)
                dve.wait_ge(stepped, base + 1)
                dve.sem_inc(passed_dve, 1)
                dve.memset(top[0:n, p, KEEP:], -1.0).then_inc(stepped, 1)
                dve.wait_ge(stepped, base + 2)
                dve.sem_inc(passed_dve, 1)
                dve.match_replace(others[0:n, :], top[0:n, p, :], near[0:n, p, :], 0.0).then_inc(stepped, 1)
                dve.wait_ge(stepped, base + 3)
                dve.tensor_tensor(near[0:n, p, 0:N], near[0:n, p, 0:N], others[0:n, 0:N], ALU.subtract) \
                    .then_inc(stepped, 1)
                dve.wait_ge(loaded[p], count(t, p))
                dve.wait_ge(stepped, base + 4)
                dve.sem_inc(passed_dve, 1)
                dve.tensor_tensor_reduce(out=adj_in[0:n, p, :], in0=near[0:n, p, 0:N], in1=adj_in[0:n, p, :],
                                         scale=1.0, scalar=0.0, op0=ALU.add, op1=ALU.add,
                                         accum_out=own_sum[0:n, p]).then_inc(graph_ready, 1)
                dve.wait_ge(graph_ready, t + 1)
                dve.tensor_copy(column_of(row_sums, t), own_sum[0:n, p]).then_inc(stepped, 1)

            def body(t, p):
                if not isinstance(t, int) or t < RT:
                    distances(t, p)
                if after(t, 1):
                    keep(t - 1, 1 - p)

            tiles(dve, body, end=RT + 1)


def store_output(nc, sem, x_rows, out):
    stored = sem("o_stored")
    with nc.Block() as block:
        @block.sync
        def _(sp):
            sp.dma_start(out[0:128 * (RT - 1)].rearrange("(t p) d -> p t d", p=128),
                         x_rows[:, 0:RT - 1, :]).then_inc(stored, 16)
            sp.dma_start(out[128 * (RT - 1):N], x_rows[0:LAST, RT - 1, :]).then_inc(stored, 16)
            sp.wait_ge(stored, 32)


def stage(nc, build, *args, **kwargs):
    held = []

    def sem(name):
        held.append(nc.alloc_semaphore(name))
        return held[-1]

    build(nc, sem, *args, **kwargs)
    nc.clear_and_free_semaphores(held)
    nc.all_engine_barrier()


def four_layers(nc, x, adj, Wq, Wk, Wv, Wo, beta, W2, b2, W3a, b3a, W3b, b3b, out, debug=None):
    def dram(name, shape, dt=fp32):
        return nc.dram_tensor(name, shape, dt, kind=(debug or {}).get(name, "Internal")).ap()

    q_planes, k_planes = dram("q_planes", [3, C, G], bf16), dram("k_planes", [3, C, G], bf16)
    v_planes, v_tiles = dram("v_planes", [C, G]), dram("v_tiles", [HEADS, 128, V_ROW])
    sums, sum_planes = dram("sums", [STEPS + LEAD, C + 1, CHUNK]), dram("sum_planes", [C + 1, G])
    graph = dram("graph", [N, N])

    stage(nc, project, x, Wq, Wk, Wv, q_planes, k_planes, v_planes)
    stage(nc, lay_out_values, v_planes, v_tiles)
    stage(nc, attention, adj, q_planes, k_planes, v_tiles, sums)
    stage(nc, gather_sums, sums, sum_planes)
    with ExitStack() as ctx:
        x_rows, y_rows, hidden = (ctx.enter_context(nc.sbuf_tensor(name, [128, RT, D], fp32))
                                  for name in ("x_rows", "y_rows", "hidden"))
        row_sums, scale = (ctx.enter_context(nc.sbuf_tensor(name, [128, RT], fp32))
                           for name in ("row_sums", "scale"))
        stage(nc, join_heads, x, sum_planes, Wo, x_rows, y_rows)
        stage(nc, layer_norm, "norm0", y_rows, x_rows)
        with ExitStack() as inner:
            gram = Gram(nc, inner, "x")
            stage(nc, prepare_gram, "x", x_rows, gram, True)
            stage(nc, cosine_attention, adj, beta, gram, x_rows, y_rows)
        stage(nc, layer_norm, "norm1", y_rows, x_rows)
        stage(nc, clear_sums, row_sums, hidden)
        stage(nc, convolve, "hop1", adj, x_rows, W2, b2, "silu", hidden, row_sums=row_sums)
        stage(nc, convolve, "hop2", adj, hidden, W2, b2, "silu_x", y_rows, x_rows=x_rows)
        stage(nc, layer_norm, "norm2", y_rows, x_rows)
        stage(nc, scale_rows, "degree1", row_sums, scale, x_rows, y_rows)
        stage(nc, convolve, "lap1", adj, y_rows, W3a, b3a, "leaky", hidden, scale=scale)
        with ExitStack() as inner:
            gram = Gram(nc, inner, "z")
            stage(nc, prepare_gram, "z", hidden, gram, False)
            stage(nc, nearest_neighbours, adj, gram, graph, row_sums)
        stage(nc, scale_rows, "degree2", row_sums, scale, x_rows, hidden)
        stage(nc, convolve, "lap2", graph, hidden, W3b, b3b, "scaled", y_rows, x_rows=x_rows, scale=scale)
        stage(nc, layer_norm, "norm3", y_rows, x_rows)
        stage(nc, store_output, x_rows, out)


def clear_sums(nc, sem, row_sums, hidden):
    cleared = sem("z_cleared")
    with nc.Block() as block:
        @block.vector
        def _(dve):
            dve.memset(row_sums[:, :], 1.0).then_inc(cleared, 1)
            dve.memset(hidden[:, :, :].rearrange("p t d -> p (t d)"), 0.0).then_inc(cleared, 1)


_INS = ["x", "adj", "L0_gnn_Wq", "L0_gnn_Wk", "L0_gnn_Wv", "L0_gnn_Wo", "L1_gnn_beta", "L2_gnn_W", "L2_gnn_b",
        "L3_gnn_W1", "L3_gnn_b1", "L3_gnn_W2", "L3_gnn_b2"]


def kernel(**inputs):
    import numpy as _np
    import concourse.bacc as _bacc
    from concourse import mybir as _mybir
    from concourse.bass_utils import run_bass_kernel_spmd as _run

    nc = _bacc.Bacc("TRN2", target_bir_lowering=False, num_devices=1)
    arrays, args = {}, []
    for name in _INS:
        a = _np.ascontiguousarray(inputs[name])
        arrays[f"in_{name}_dram"] = a
        args.append(nc.dram_tensor(f"in_{name}_dram", a.shape, _mybir.dt.from_np(a.dtype),
                                   kind="ExternalInput").ap())
    out = nc.dram_tensor("out_0_dram", (N, D), _mybir.dt.float32, kind="ExternalOutput").ap()
    four_layers(nc, *args, out)
    return _run(nc, [arrays], core_ids=[0]).results[0]["out_0_dram"]
```

```python
import concourse.bass as bass
from concourse import mybir
from contextlib import ExitStack

fp32 = mybir.dt.float32
bf16 = mybir.dt.bfloat16
ALU = mybir.AluOpType
ACT = mybir.ActivationFunctionType
AX = mybir.AxisListType

N, D = 3327, 128
HEADS, C = 128, 8
FEAT = HEADS * C
G = N * HEADS
RT = -(-N // 128)
LAST = N - 128 * (RT - 1)
LOWEST = -3.0e38


def width(t):
    return 128 if not isinstance(t, int) or t < RT - 1 else LAST


def after(t, n):
    return not isinstance(t, int) or t >= n


def tiles(eng, body, end=RT):
    for t in range(2):
        body(t, t % 2)
    with eng.Fori(1, RT // 2 - 1) as pair:
        for p in range(2):
            body(pair * 2 + p, p)
    for t in range(RT - 2, end):
        body(t, t % 2)


def count(t, p, each=16):
    return (t - p) * (each // 2) + each


def node_rows(t):
    return bass.ds(t * 128, width(t))


def row_of(buffer, t):
    n = width(t)
    if isinstance(t, int):
        return buffer[0:n, t, :]
    return buffer[:, bass.ds(t, 1), :].rearrange("p o n -> p (o n)")


def banks(n, size=512):
    return [(a, min(size, n - a)) for a in range(0, n, size)]




def write_identity(nc, pool, ident, done):
    pool.memset(ident[:, :], 0.0).then_inc(done, 1)
    pool.wait_ge(done, 1)
    pool.affine_select(out=ident[:, :], in_=ident[:, :], compare_op=ALU.not_equal, fill=1.0, base=0,
                       pattern=[[-1, 128]], channel_multiplier=1).then_inc(done, 1)


def project(nc, sem, x, Wq, Wk, Wv, q_planes, k_planes, v_planes):
    Q_SCALE = 0.5 * float(D) ** -0.5
    with ExitStack() as ctx:
        def sb(name, shape, dt=fp32):
            return ctx.enter_context(nc.sbuf_tensor(name, shape, dt))

        x_in = sb("p_x_in", [128, 2, D])
        w_in = sb("p_w_in", [128, 3, C, D])
        w_t = sb("p_w_t", [128, 3, C, 128])
        xt = sb("p_xt", [128, 2, 128])
        ident = sb("p_ident", [128, 128])
        full = sb("p_full", [128, 2, 3, FEAT])
        rest = sb("p_rest", [128, 2, FEAT])
        part = sb("p_part", [128, 2, 2, 3, FEAT], bf16)
        turn = ctx.enter_context(nc.psum_tensor("p_turn", [128, 2, 512], fp32))
        proj = ctx.enter_context(nc.psum_tensor("p_proj", [128, 3, 2, 512], fp32))

        ident_made = sem("p_ident_made")
        w_loaded = sem("p_w_loaded")
        x_loaded = [sem(f"p_x_loaded{i}") for i in range(2)]
        w_turned = sem("p_w_turned")
        w_copied = sem("p_w_copied")
        x_turned = sem("p_x_turned")
        x_copied = sem("p_x_copied")
        projected = sem("p_projected")
        taken = sem("p_taken")
        q_split = sem("p_q_split")
        k_split = sem("p_k_split")
        stored = [sem(f"p_stored{i}") for i in range(2)]
        passed_dve, passed_pool = sem("p_passed_dve"), sem("p_passed_pool")
        passed_sp = sem("p_passed_sp")

        PARTS = 5
        STORES = 16 * 7
        block = ctx.enter_context(nc.Block())

        @block.sync
        def _(sp):
            for m, w in enumerate((Wq, Wk, Wv)):
                sp.dma_start(w_in[:, m], w.rearrange("(j c) d -> j c d", c=C)).then_inc(w_loaded, 16)

            def store(t, p):
                n = width(t)
                rows = bass.ds(t * (128 * 128), n * 128)
                sp.wait_ge(taken, t * 3 + 3)
                sp.sem_inc(passed_sp, 1)
                sp.dma_start(v_planes[:, rows].rearrange("c (m j) -> m c j", j=128),
                             full[0:n, p, 2].rearrange("m (c j) -> m c j", c=C)).then_inc(stored[p], 16)
                for m, (planes, split) in enumerate(((q_planes, q_split), (k_planes, k_split))):
                    sp.wait_ge(split, t * PARTS + PARTS)
                    sp.sem_inc(passed_sp, 1)
                    for s in range(3):
                        sp.dma_start(planes[s, :, rows].rearrange("c (m j) -> m c j", j=128),
                                     part[0:n, p, m, s].rearrange("m (c j) -> m c j", c=C)) \
                            .then_inc(stored[p], 16)

            def body(t, p):
                if after(t, 2):
                    sp.wait_ge(x_turned, t - 1)
                    sp.sem_inc(passed_sp, 1)
                sp.dma_start(x_in[0:width(t), p], x[node_rows(t)]).then_inc(x_loaded[p], 16)
                if after(t, 1):
                    store(t - 1, 1 - p)

            tiles(sp, body)
            store(RT - 1, 1)
            for p in range(2):
                sp.wait_ge(stored[p], STORES * RT // 2)

        @block.tensor
        def _(pe):
            pe.wait_ge(ident_made, 2)
            pe.wait_ge(w_loaded, 48)
            for i in range(6):
                m, c0 = i // 2, 4 * (i % 2)
                if i >= 2:
                    pe.wait_ge(w_copied, i - 1)
                for c in range(4):
                    mm = pe.transpose(turn[:, i % 2, c * 128:c * 128 + 128], w_in[:, m, c0 + c], ident[:, :])
                mm.then_inc(w_turned, 1)
            pe.wait_ge(w_copied, 6)

            def body(t, p):
                n = width(t)
                pe.wait_ge(x_loaded[p], count(t, p))
                if after(t, 2):
                    pe.wait_ge(x_copied, t - 1)
                pe.transpose(turn[:, p, 0:n], x_in[0:n, p], ident[0:n, 0:n]).then_inc(x_turned, 1)
                pe.wait_ge(x_copied, t + 1)
                for m in range(3):
                    if after(t, 1):
                        pe.wait_ge(taken, t * 3 + (m - 2))
                    for b in range(2):
                        mm = pe.matmul(proj[0:n, m, b], xt[:, p, 0:n],
                                       w_t[:, m, 4 * b:4 * b + 4].rearrange("d c j -> d (c j)"),
                                       start=True, stop=True)
                    mm.then_inc(projected, 1)

            tiles(pe, body)

        @block.scalar
        def _(act):
            def body(t, p):
                n = width(t)
                for m, scale in enumerate((Q_SCALE, 1.0, 1.0)):
                    act.wait_ge(projected, t * 3 + (m + 1))
                    if after(t, 2) and m == 0:
                        act.wait_ge(stored[p], count(t - 2, p, STORES))
                        act.wait_ge(q_split, t * PARTS - PARTS)
                        act.wait_ge(k_split, t * PARTS - PARTS)
                    act.activation(full[0:n, p, m], proj[0:n, m].rearrange("m b c -> m (b c)"),
                                   ACT.Copy, scale=scale).then_inc(taken, 1)

            tiles(act, body)

        def split(eng, m, done, passed, t, p):
            n = width(t)
            src, left, out = full[0:n, p, m], rest[0:n, m], part[0:n, p, m]
            eng.wait_ge(taken, t * 3 + (m + 1))
            eng.sem_inc(passed, 1)
            if after(t, 2):
                eng.wait_ge(stored[p], count(t - 2, p, STORES))
                eng.sem_inc(passed, 1)
            steps = [lambda: eng.tensor_copy(out[:, 0], src),
                     lambda: eng.tensor_tensor(left, src, out[:, 0], ALU.subtract),
                     lambda: eng.tensor_copy(out[:, 1], left),
                     lambda: eng.tensor_tensor(left, left, out[:, 1], ALU.subtract),
                     lambda: eng.tensor_copy(out[:, 2], left)]
            for i, step in enumerate(steps):
                step().then_inc(done, 1)
                eng.wait_ge(done, t * PARTS + (i + 1))
                eng.sem_inc(passed, 1)

        @block.vector
        def _(dve):
            for i in range(6):
                dve.wait_ge(w_turned, i + 1)
                m, c0 = i // 2, 4 * (i % 2)
                dve.tensor_copy(w_t[:, m, c0:c0 + 4].rearrange("d c j -> d (c j)"), turn[:, i % 2]) \
                    .then_inc(w_copied, 1)

            def body(t, p):
                n = width(t)
                dve.wait_ge(x_turned, t + 1)
                if after(t, 2):
                    dve.wait_ge(projected, t * 3 - 3)
                dve.tensor_copy(xt[:, p, 0:n], turn[:, p, 0:n]).then_inc(x_copied, 1)
                split(dve, 0, q_split, passed_dve, t, p)

            tiles(dve, body)

        @block.gpsimd
        def _(pool):
            write_identity(nc, pool, ident, ident_made)
            tiles(pool, lambda t, p: split(pool, 1, k_split, passed_pool, t, p))


PAIR_C = 2 * (C + 1)
V_ROW = RT * PAIR_C


def lay_out_values(nc, sem, v_planes, v_tiles):
    HG = 128 // C
    GROUPS = HEADS // HG
    with ExitStack() as ctx:
        planes = ctx.enter_context(nc.sbuf_tensor("v_planes_in", [128, 2, N], fp32))
        tiles = ctx.enter_context(nc.sbuf_tensor("v_tiles_out", [128, 2, HG, RT, PAIR_C], fp32))
        ident = ctx.enter_context(nc.sbuf_tensor("v_ident", [128, 128], fp32))
        turn = ctx.enter_context(nc.psum_tensor("v_turn", [128, 4, 512], fp32))
        ident_made, turned = sem("v_ident_made"), sem("v_turned")
        loaded = [sem(f"v_loaded{i}") for i in range(2)]
        copied = [sem("v_copied_even"), sem("v_copied_odd")]
        ones_made = sem("v_ones_made")
        stored = [sem(f"v_stored{i}") for i in range(2)]
        block = ctx.enter_context(nc.Block())

        def store(sp, g):
            for odd in range(2):
                sp.wait_ge(copied[odd], RT // 2 * (g + 1))
            sp.wait_ge(ones_made, 3)
            sp.dma_start(v_tiles[g * HG:g * HG + HG].rearrange("h p n -> p h n"),
                         tiles[:, g % 2].rearrange("p h t c -> p h (t c)")).then_inc(stored[g % 2], 16)

        def copy_tiles(eng, copy, odd):
            for g in range(GROUPS):
                if g >= 2:
                    eng.wait_ge(stored[g % 2], 16 * (g // 2))
                for t in range(odd, RT, 2):
                    u = g * RT + t
                    eng.wait_ge(turned, u + 1)
                    values = turn[0:width(t), u % 4, 0:128].rearrange("p (h c) -> p h c", c=C)
                    for head in range(2):
                        c = head * (C + 1)
                        write = copy(tiles[0:width(t), g % 2, head::2, t, c:c + C], values[:, head::2])
                    write.then_inc(copied[odd], 1)

        @block.sync
        def _(sp):
            for g in range(GROUPS):
                if g >= 2:
                    sp.wait_ge(turned, RT * (g - 1))
                for h in range(HG):
                    start = (g * HG + h) * N
                    sp.dma_start(planes[h * C:h * C + C, g % 2], v_planes[:, start:start + N]) \
                        .then_inc(loaded[g % 2], 16)
                if g >= 1:
                    store(sp, g - 1)
            store(sp, GROUPS - 1)
            for p in range(2):
                sp.wait_ge(stored[p], 16 * GROUPS // 2)

        @block.gpsimd
        def _(pool):
            write_identity(nc, pool, ident, ident_made)

        @block.tensor
        def _(pe):
            pe.wait_ge(ident_made, 2)
            for g in range(GROUPS):
                pe.wait_ge(loaded[g % 2], 16 * HG * (g // 2 + 1))
                for t in range(RT):
                    u = g * RT + t
                    if u >= 4:
                        pe.wait_ge(copied[u % 2], u // 2 - 1)
                    pe.transpose(turn[0:width(t), u % 4, 0:128], planes[:, g % 2, t * 128:t * 128 + width(t)],
                                 ident[:, :]).then_inc(turned, 1)

        @block.vector
        def _(dve):
            dve.memset(tiles[:, :, :, :, :].rearrange("p b h t c -> p (b h t c)"), 0.0).then_inc(ones_made, 1)
            dve.wait_ge(ones_made, 1)
            for odd in range(2):
                c = odd * (C + 1) + C
                for slot in range(2):
                    write = dve.memset(tiles[:, slot, odd::2, :, c:c + 1], 1.0)
                write.then_inc(ones_made, 1)
            copy_tiles(dve, dve.tensor_copy, 0)

        @block.scalar
        def _(act):
            act.wait_ge(ones_made, 3)
            copy_tiles(act, lambda out, in_: act.activation(out, in_, ACT.Copy), 1)


CHUNKS = 7
CSTEP = 475
CHUNK = N - (CHUNKS - 1) * CSTEP
assert CSTEP <= CHUNK <= 512
SUBS = [(a, min(120, CHUNK - a)) for a in range(0, CHUNK, 120)]
KROWS = 9 * C
KPAD = 96
assert KROWS <= KPAD and HEADS % 2 == 0
STEPS = CHUNKS * HEADS
LEAD = 4

PE_ORDER = """
    S0:0 T21:2 T22:2 M4:2 T23:2 S1:0 S2:0 T24:2 T25:2 M5:2 S3:0 T0:1 T1:1 M6:2 S4:0 T2:1 S5:0 T3:1 T4:1
    T5:1 S6:0 M0:1 S7:0 T6:1 T7:1 T8:1 S8:0 S9:0 U0:2 M1:1 T9:1 T10:1 S10:0 T11:1 T12:1 S11:0 T13:1
    T14:1 S12:0 M2:1 S13:0 T15:1 T16:1 S14:0 T17:1 T18:1 S15:0 M3:1 T19:1 T20:1"""
DVE_ORDER = """
    E20:2 A0:0 E22:2 E23:2 A1:0 A2:0 A3:0 R0:0 P0:2 A4:0 A5:0 E5:1 A6:0 A7:0 E6:1 A8:0 R1:0 A9:0 A10:0
    A11:0 E12:1 E13:1 A12:0 R2:0 A13:0 A14:0 A15:0 E18:1 E19:1 R3:0"""
ACT_ORDER = """
    X2:1 E21:2 X3:1 E24:2 E25:2 E0:1 E1:1 E2:1 E3:1 E4:1 X0:0 E7:1 E8:1 O0:2 E9:1 E10:1 E11:1 X1:0 E14:1
    E15:1 E16:1 E17:1"""


def ordered(text):
    return [(word[0], int(word[1:].split(":")[0]), int(word.split(":")[1])) for word in text.split()]


def attention(nc, sem, adj, q_planes, k_planes, v_tiles, sum_planes):
    with ExitStack() as ctx:
        def sb(name, shape, dt=fp32):
            return ctx.enter_context(nc.sbuf_tensor(name, shape, dt))

        def psum(name, shape):
            return ctx.enter_context(nc.psum_tensor(name, shape, fp32))

        NS = len(SUBS)
        UNITS = banks(N, 1024)
        NU = len(UNITS) * NS
        GROUPS = -(-RT // 4)
        PAIR_TILES = 2 * RT
        assert PAIR_TILES % 4 == 0 and RT % 4 == 2
        RING = 8
        pe_order, dve_order, act_order = ordered(PE_ORDER), ordered(DVE_ORDER), ordered(ACT_ORDER)
        BY_DVE = [i for kind, i, _ in sorted(dve_order) if kind == "E"]
        BY_ACT = [i for kind, i, _ in sorted(act_order) if kind == "E"]
        assert sorted(BY_DVE + BY_ACT) == list(range(RT))
        turns = [(kind, i, lag) for kind, i, lag in pe_order if kind in "TU"]
        bank = {(kind, i): n % 3 for n, (kind, i, _) in enumerate(turns)}
        assert len(turns) == RT + 1 and len(turns) % 3 == 0
        BY_PAIR = "PUO"

        k_op = [sb(f"a_k{i}", [KPAD, N], bf16) for i in range(2)]
        q_op = [sb(f"a_q{i}", [KPAD, CHUNK], bf16) for i in range(2)]
        v_op = [sb(f"a_v{i}", [128, RT, PAIR_C]) for i in range(2)]
        adj_rows = sb("a_adj", [120, NS, N])
        probs = [sb(f"a_probs{i}", [120, NS, N]) for i in range(2)]
        unit_max = sb("a_unit_max", [120, 2, NS, len(UNITS)])
        neg_max = sb("a_neg_max", [120, 2, NS])
        probs_t = sb("a_probs_t", [128, RING, CHUNK])
        partial = sb("a_partial", [128, CHUNK])
        total = sb("a_total", [PAIR_C, CHUNK])
        ident = sb("a_ident", [128, 128])
        select = sb("a_select", [128, PAIR_C])
        score = [psum(f"a_score{i}", [128, 1024]) for i in range(2)]
        turn = psum("a_turn", [128, 3, 512])
        acc = psum("a_acc", [128, 512])

        ident_made, select_made = sem("a_ident_made"), sem("a_select_made")
        adj_loaded = sem("a_adj_loaded")
        qk_loaded = [sem(f"a_qk_loaded{i}") for i in range(2)]
        v_loaded = [sem(f"a_v_loaded{i}") for i in range(2)]
        scored = sem("a_scored")
        unit_done = sem("a_unit_done")
        max_ready = sem("a_max_ready")
        probs_ready = sem("a_probs_ready")
        turned = sem("a_turned")
        emptied_dve, emptied_act = sem("a_emptied_dve"), sem("a_emptied_act")
        multiplied = sem("a_multiplied")
        acc_zeroed = sem("a_acc_zeroed")
        acc_taken = sem("a_acc_taken")
        summed = sem("a_summed")
        total_ready = sem("a_total_ready")
        total_zeroed = sem("a_total_zeroed")
        stored = sem("a_stored")
        padded = sem("a_padded")
        passed_dve, passed_sp = sem("a_passed_dve"), sem("a_passed_sp")

        def units_scored(t, u):
            return t * NU + (2 * NU + u)

        def groups_multiplied(h, g):
            return h * GROUPS + (2 * GROUPS + g)

        def group_of(h, p, place):
            if place < 0:
                v = place + RING
                place = max(last for last in range(PAIR_TILES) if last % RING == v)
                return groups_multiplied(h - 1, (place - RT + 2) // 4 + 1)
            if place < RT - 2:
                return groups_multiplied(h - p, place // 4 + 1)
            return groups_multiplied(h + 1 - p, (place - RT + 2) // 4 + 1)

        def plan(order, t, p):
            for kind, i, lag in order:
                if kind in BY_PAIR and (p - lag) % 2 == 0:
                    continue
                if not isinstance(t, int) or 0 <= t - lag < STEPS:
                    yield kind, i, t - lag, (p - lag) % 2

        def emptied(eng, head, v):
            if v in BY_DVE:
                eng.wait_ge(emptied_dve, len(BY_DVE) * head + sum(w <= v for w in BY_DVE))
            else:
                eng.wait_ge(emptied_act, len(BY_ACT) * head + sum(w <= v for w in BY_ACT))

        def steps(eng, body):
            for t in range(2):
                body(t, t % 2)
            with eng.Fori(1, STEPS // 2) as pair:
                for p in range(2):
                    body(pair * 2 + p, p)
            for t in range(STEPS, STEPS + 2):
                body(t, t % 2)

        block = ctx.enter_context(nc.Block())

        @block.sync
        def _(sp):
            sp.wait_ge(padded, 4)

            def load(chunk, head, p, first=False):
                sp.wait_ge(scored, units_scored(chunk * HEADS + head - 1, 0))
                for s in range(3):
                    for r in range(3):
                        at = s * 3 * C + r * C
                        sp.dma_start(k_op[p][at:at + C, :], k_planes[s, :, bass.ds(head * N, N)]) \
                            .then_inc(qk_loaded[p], 16)
                    if first and s == 2:
                        sp.wait_ge(adj_loaded, chunk * (16 * NS) + 16 * NS)
                        sp.sem_inc(passed_sp, 1)
                    sp.dma_start(q_op[p][s * 3 * C:(s + 1) * 3 * C, :],
                                 q_planes.rearrange("s c n -> (s c) n")
                                 [:, bass.ds(head * N + chunk * CSTEP, CHUNK)]).then_inc(qk_loaded[p], 16)

            def store(step, start):
                sp.wait_ge(total_ready, step + 2)
                sp.sem_inc(passed_sp, 1)
                for odd in range(2):
                    sp.dma_start(sum_planes[:, bass.ds(start + odd * N, CHUNK)],
                                 total[odd * (C + 1):(odd + 1) * (C + 1), :]).then_inc(stored, 16)

            def load_and_store(chunk, pair, start):
                load(chunk, pair * 2, 0, first=isinstance(pair, int) and pair == 0)
                store(chunk * HEADS + pair * 2, start)
                load(chunk, pair * 2 + 1, 1)

            sp.wait_ge(total_zeroed, 1)
            with sp.Fori(0, CHUNKS) as chunk:
                for pair in range(LEAD // 2):
                    load_and_store(chunk, pair, chunk * CSTEP + ((HEADS - LEAD + 2 * pair) * N - CSTEP))
                with sp.Fori(LEAD // 2, HEADS // 2) as pair:
                    load_and_store(chunk, pair, pair * (2 * N) + (chunk * CSTEP - LEAD * N))
            for i in range(LEAD // 2):
                store(STEPS + 2 * i, (CHUNKS - 1) * CSTEP + (HEADS - LEAD + 2 * i) * N)
                sp.wait_ge(stored, 16 * (STEPS + 2 * i + 2))

        @block.gpsimd
        def _(pool):
            write_identity(nc, pool, ident, ident_made)
            pool.memset(select[:, :], 0.0).then_inc(select_made, 1)
            for j in range(4):
                pool.wait_ge(select_made, j + 1)
                pool.affine_select(out=select[:, :], in_=select[:, :], compare_op=ALU.not_equal, fill=1.0,
                                   base=-32 * j, pattern=[[-1, PAIR_C]], channel_multiplier=1) \
                    .then_inc(select_made, 1)

            def load_adj(chunk, first=False):
                for s, (a, w) in enumerate(SUBS):
                    if not first:
                        pool.wait_ge(unit_done, chunk * (HEADS * NU) - (NU - NU // NS * (s + 1)))
                    pool.dma_start(adj_rows[0:w, s, :], adj[bass.ds(chunk * CSTEP + a, w)]) \
                        .then_inc(adj_loaded, 16)

            def load_values(chunk):
                with pool.Fori(0, HEADS // 2) as pair:
                    for p in range(2):
                        head = pair * 2 + p
                        pool.wait_ge(multiplied, groups_multiplied(chunk * HEADS + head - 1, 1 - p))
                        pool.dma_start(v_op[p][:, :, :].rearrange("p t c -> p (t c)"),
                                       v_tiles[bass.ds(head, 1)].rearrange("o p n -> (o p) n")) \
                            .then_inc(v_loaded[p], 16)

            load_adj(0, first=True)
            with pool.Fori(0, CHUNKS - 1) as chunk:
                load_values(chunk)
                load_adj(chunk + 1)
            load_values(CHUNKS - 1)

        @block.tensor
        def _(pe):
            pe.sem_inc(scored, 2 * NU)
            pe.sem_inc(multiplied, 2 * GROUPS)
            pe.sem_inc(summed, 2)
            pe.sem_inc(acc_taken, 2)
            pe.wait_ge(ident_made, 2)
            pe.wait_ge(select_made, 5)

            def score_unit(t, p, u):
                s, j = divmod(u, len(UNITS))
                w, (m0, mw) = SUBS[s][1], UNITS[j]
                if u == 0:
                    pe.wait_ge(qk_loaded[p], 16 * 12 * (t // 2 + 1) if isinstance(t, int)
                               else (t - p) * 96 + 192)
                if not isinstance(t, int) or t * NU + u >= 2:
                    pe.wait_ge(unit_done, t * NU + u - 1)
                for a, n in banks(mw):
                    mm = pe.matmul(score[u % 2][0:w, a:a + n], q_op[p][:, SUBS[s][0]:SUBS[s][0] + w],
                                   k_op[p][:, m0 + a:m0 + a + n], start=True, stop=True)
                mm.then_inc(scored, 1)

            def turn_free(t, p, kind, i):
                n = [user[:2] for user in turns].index((kind, i))
                back = 3
                before, j, lag = turns[n - back]
                if before == "U" and (p - lag - (n < back)) % 2 == 0:
                    back = 6
                    before, j, lag = turns[n - back]
                head = t - lag - (n < back)
                if isinstance(t, int) and not 0 <= head < STEPS:
                    return
                if before == "T":
                    emptied(pe, head, j)
                else:
                    pe.wait_ge(total_ready, head + (LEAD + 1))

            def turn_tile(t, step_parity, h, p, v):
                if v == 0:
                    pe.wait_ge(probs_ready, h * NS + NS)
                turn_free(t, step_parity, "T", v)
                n = width(v)
                for s, (a, w) in enumerate(SUBS):
                    mm = pe.transpose(turn[0:n, bank["T", v], a:a + w], probs[p][0:w, s, v * 128:v * 128 + n],
                                      ident[0:w, 0:w])
                mm.then_inc(turned, 1)

            def multiply(h, p, g):
                first = 4 * g + p * (RT - 2)
                group = [(h - p + place // RT, place // RT, place % RT) for place in range(first, first + 4)]
                for owner in (BY_DVE, BY_ACT):
                    for head, _, v in [tile for tile in group if tile[2] in owner][-1:]:
                        emptied(pe, head, v)
                if g == 0:
                    pe.wait_ge(v_loaded[p], 16 * (h // 2 + 1) if isinstance(h, int) else (h - p) * 8 + 16)
                    pe.wait_ge(acc_zeroed, 1)
                    if p == 0:
                        pe.wait_ge(acc_taken, h + 2)
                for place, (_, odd, v) in enumerate(group, first):
                    n = width(v)
                    mm = pe.matmul(acc[32 * (place % 4):32 * (place % 4) + PAIR_C, 0:CHUNK], v_op[odd][0:n, v, :],
                                   probs_t[0:n, place % RING, :], start=(place < 4),
                                   stop=(place >= PAIR_TILES - 4))
                mm.then_inc(multiplied, 2 if (p, g) == (0, GROUPS - 2) else 1)

            def add_up(t, step_parity, h):
                pe.wait_ge(acc_taken, h + 3)
                turn_free(t, step_parity, "U", 0)
                pe.matmul(turn[0:PAIR_C, bank["U", 0], 0:CHUNK], select[:, :], partial[:, :],
                          start=True, stop=True).then_inc(summed, 2)

            def body(t, p):
                for kind, i, head, parity in plan(pe_order, t, p):
                    if kind == "S":
                        score_unit(head, parity, i)
                    elif kind == "T":
                        turn_tile(t, p, head, parity, i)
                    elif kind == "M":
                        if (parity, i) != (0, GROUPS - 1):
                            multiply(head, parity, i)
                    else:
                        add_up(t, p, head)

            steps(pe, body)

        def empty_tile(eng, h, p, v):
            n, place = width(v), p * RT + v
            eng.wait_ge(turned, h * RT + v + 1)
            if place >= RING or not isinstance(h, int) or h > 0:
                eng.wait_ge(multiplied, group_of(h, p, place - RING))
            out, in_ = probs_t[0:n, place % RING, :], turn[0:n, bank["T", v], 0:CHUNK]
            if v in BY_DVE:
                eng.tensor_copy(out, in_).then_inc(emptied_dve, 1)
            else:
                eng.activation(out, in_, ACT.Copy).then_inc(emptied_act, 1)

        @block.vector
        def _(dve):
            dve.memset(acc[:, :], 0.0).then_inc(acc_zeroed, 1)
            for op in (*k_op, *q_op):
                dve.memset(op[64:KPAD, :], 0.0).then_inc(padded, 1)
            dve.memset(total[:, :], 0.0).then_inc(total_zeroed, 1)
            dve.wait_ge(total_zeroed, 1)
            dve.sem_inc(total_ready, LEAD)

            def add_adj(t, p, u):
                s, j = divmod(u, len(UNITS))
                w, (m0, mw) = SUBS[s][1], UNITS[j]
                dve.wait_ge(scored, units_scored(t, u + 1))
                if s == 0 and after(t, 2):
                    dve.wait_ge(turned, t * RT - 2 * RT + min(RT, -(-(m0 + mw) // 128)))
                dve.sem_inc(passed_dve, 1)
                dve.tensor_tensor_reduce(out=probs[p][0:w, s, m0:m0 + mw], in0=score[u % 2][0:w, 0:mw],
                                         in1=adj_rows[0:w, s, m0:m0 + mw], scale=2.0, scalar=LOWEST,
                                         op0=ALU.add, op1=ALU.max, accum_out=unit_max[0:w, p, s, j:j + 1]) \
                    .then_inc(unit_done, 1)

            def greatest(t, p, s):
                w = SUBS[s][1]
                dve.wait_ge(unit_done, t * NU + (s + 1) * len(UNITS))
                dve.tensor_reduce(out=neg_max[0:w, p, s:s + 1], in_=unit_max[0:w, p, s, :], axis=AX.X,
                                  op=ALU.max, negate=True).then_inc(max_ready, 1)

            def take_partial(h):
                dve.wait_ge(multiplied, groups_multiplied(h, GROUPS))
                dve.wait_ge(summed, h + 1)
                dve.tensor_copy(partial[:, :], acc[:, 0:CHUNK]).then_inc(acc_taken, 2)

            def body(t, p):
                for kind, i, head, parity in plan(dve_order, t, p):
                    if kind == "A":
                        add_adj(head, parity, i)
                    elif kind == "R":
                        greatest(head, parity, i)
                    elif kind == "E":
                        empty_tile(dve, head, parity, i)
                    else:
                        take_partial(head)

            steps(dve, body)

        @block.scalar
        def _(act):
            def exponentials(h, p, s):
                w = SUBS[s][1]
                act.wait_ge(max_ready, h * NS + s + 1)
                act.activation(probs[p][0:w, s, :], probs[p][0:w, s, :], ACT.Exp,
                               bias=neg_max[0:w, p, s:s + 1]).then_inc(probs_ready, 1)

            def take_total(h):
                act.wait_ge(summed, h + 3)
                act.wait_ge(stored, h * 16 + 48)
                act.wait_ge(total_zeroed, 1)
                act.activation(total[:, :], turn[0:PAIR_C, bank["U", 0], 0:CHUNK], ACT.Copy) \
                    .then_inc(total_ready, 2)

            def body(t, p):
                for kind, i, head, parity in plan(act_order, t, p):
                    if kind == "X":
                        exponentials(head, parity, i)
                    elif kind == "E":
                        empty_tile(act, head, parity, i)
                    else:
                        take_total(head)

            steps(act, body)


def join_heads(nc, sem, x, sum_planes, Wo, x_rows, y_rows):
    with ExitStack() as ctx:
        def sb(name, shape, dt=fp32):
            return ctx.enter_context(nc.sbuf_tensor(name, shape, dt))

        planes = sb("j_planes", [128, 2, C + 1, 128])
        inverse = sb("j_inverse", [128, 2, 128])
        heads = sb("j_heads", [128, 2, C, 128])
        heads_t = sb("j_heads_t", [128, 2, C, 128])
        wo_in = sb("j_wo_in", [128, FEAT])
        wo_t = sb("j_wo_t", [128, C, D])
        ident = sb("j_ident", [128, 128])
        turn = ctx.enter_context(nc.psum_tensor("j_turn", [128, 2, 2, 512], fp32))
        joined = ctx.enter_context(nc.psum_tensor("j_joined", [128, 2, 512], fp32))
        ident_made, x_loaded, wo_loaded = sem("j_ident_made"), sem("j_x_loaded"), sem("j_wo_loaded")
        y_zeroed, wo_turned, wo_copied = sem("j_y_zeroed"), sem("j_wo_turned"), sem("j_wo_copied")
        loaded = [sem(f"j_loaded{i}") for i in range(2)]
        inverted, scaled, turned = sem("j_inverted"), sem("j_scaled"), sem("j_turned")
        copied, multiplied, added = sem("j_copied"), sem("j_multiplied"), sem("j_added")
        block = ctx.enter_context(nc.Block())

        @block.sync
        def _(sp):
            sp.dma_start(wo_in[:, :], Wo).then_inc(wo_loaded, 16)
            sp.wait_ge(y_zeroed, 2)
            sp.dma_start(x_rows[:, 0:RT - 1, :], x[0:128 * (RT - 1)].rearrange("(t p) d -> p t d", p=128)) \
                .then_inc(x_loaded, 16)
            sp.dma_start(x_rows[0:LAST, RT - 1, :], x[128 * (RT - 1):N]).then_inc(x_loaded, 16)

            def body(t, p):
                if after(t, 2):
                    sp.wait_ge(scaled, t - 1)
                sp.dma_start(planes[0:width(t), p], sum_planes[:, bass.ds(t * (128 * 128), width(t) * 128)]
                             .rearrange("c (r j) -> r c j", j=128)).then_inc(loaded[p], 16)

            tiles(sp, body)

        @block.gpsimd
        def _(pool):
            write_identity(nc, pool, ident, ident_made)

        @block.tensor
        def _(pe):
            pe.wait_ge(ident_made, 2)
            pe.wait_ge(wo_loaded, 16)
            for c in range(C):
                mm = pe.transpose(turn[:, 0, c // 4, c % 4 * 128:c % 4 * 128 + 128], wo_in[:, c:FEAT:C],
                                  ident[:, :])
            mm.then_inc(wo_turned, 1)
            pe.wait_ge(wo_copied, 1)

            def body(t, p):
                n = width(t)
                pe.wait_ge(scaled, t + 1)
                if after(t, 2):
                    pe.wait_ge(copied, t - 1)
                for c in range(C):
                    mm = pe.transpose(turn[:, p, c // 4, c % 4 * 128:c % 4 * 128 + n], heads[0:n, p, c],
                                      ident[0:n, 0:n])
                mm.then_inc(turned, 1)
                pe.wait_ge(copied, t + 1)
                if after(t, 2):
                    pe.wait_ge(added, t - 1)
                for c in range(C):
                    mm = pe.matmul(joined[0:n, p, 0:D], heads_t[:, p, c, 0:n], wo_t[:, c, :],
                                   start=(c == 0), stop=(c == C - 1))
                mm.then_inc(multiplied, 1)

            tiles(pe, body)

        @block.scalar
        def _(act):
            def body(t, p):
                n = width(t)
                act.wait_ge(turned, t + 1)
                if after(t, 2):
                    act.wait_ge(multiplied, t - 1)
                act.activation(heads_t[:, p, :, 0:n],
                               turn[:, p].rearrange("j b (c r) -> j (b c) r", c=4)[:, :, 0:n], ACT.Copy) \
                    .then_inc(copied, 1)

            tiles(act, body)

        @block.vector
        def _(dve):
            dve.memset(x_rows[:, :, :].rearrange("p t d -> p (t d)"), 0.0).then_inc(y_zeroed, 1)
            dve.memset(y_rows[:, :, :].rearrange("p t d -> p (t d)"), 0.0).then_inc(y_zeroed, 1)
            dve.wait_ge(wo_turned, 1)
            dve.tensor_copy(wo_t[:, :, :].rearrange("j c e -> j (c e)"),
                            turn[:, 0].rearrange("j b n -> j (b n)")).then_inc(wo_copied, 1)
            dve.wait_ge(x_loaded, 32)

            def add(t, p):
                dve.wait_ge(multiplied, t + 1)
                dve.tensor_tensor(row_of(y_rows, t), joined[0:width(t), p, 0:D], row_of(x_rows, t), ALU.add) \
                    .then_inc(added, 1)

            def body(t, p):
                n = width(t)
                dve.wait_ge(loaded[p], count(t, p))
                dve.reciprocal(inverse[0:n, p], planes[0:n, p, C]).then_inc(inverted, 1)
                if after(t, 2):
                    dve.wait_ge(turned, t - 1)
                dve.wait_ge(inverted, t + 1)
                dve.tensor_tensor(heads[0:n, p], planes[0:n, p, 0:C],
                                  inverse[0:n, p].unsqueeze(1).broadcast_to([n, C, 128]), ALU.mult) \
                    .then_inc(scaled, 1)
                if after(t, 1):
                    add(t - 1, 1 - p)

            tiles(dve, body)
            add(RT - 1, 1)


def layer_norm(nc, sem, tag, y_rows, x_rows):
    with ExitStack() as ctx:
        total = ctx.enter_context(nc.sbuf_tensor(f"{tag}_total", [128, RT], fp32))
        scale = ctx.enter_context(nc.sbuf_tensor(f"{tag}_scale", [128, RT], fp32))
        stepped, rooted = sem(f"{tag}_stepped"), sem(f"{tag}_rooted")
        block = ctx.enter_context(nc.Block())

        def spread(small):
            return small[:, :].unsqueeze(2).broadcast_to([128, RT, D])

        @block.scalar
        def _(act):
            act.wait_ge(stepped, 6)
            act.activation(scale[:, :], total[:, :], ACT.Sqrt).then_inc(rooted, 1)

        @block.vector
        def _(dve):
            x, y = x_rows[:, :, :], y_rows[:, :, :]
            steps = [
                lambda: dve.tensor_reduce(out=total[:, :], in_=y, axis=AX.X, op=ALU.add),
                lambda: dve.tensor_scalar(total[:, :], total[:, :], 1.0 / D, None, ALU.mult),
                lambda: dve.tensor_tensor(y, y, spread(total), ALU.subtract),
                lambda: dve.tensor_tensor(x, y, y, ALU.mult),
                lambda: dve.tensor_reduce(out=total[:, :], in_=x, axis=AX.X, op=ALU.add),
                lambda: dve.tensor_scalar(total[:, :], total[:, :], 1.0 / D, 1e-5, ALU.mult, ALU.add),
                lambda: dve.reciprocal(scale[:, :], scale[:, :]),
                lambda: dve.tensor_tensor(x, y, spread(scale), ALU.mult),
            ]
            for i, step in enumerate(steps):
                if i == 6:
                    dve.wait_ge(rooted, 1)
                step().then_inc(stepped, 1)
                dve.wait_ge(stepped, i + 1)


class Gram:
    def __init__(self, nc, ctx, tag):
        self.xt = ctx.enter_context(nc.sbuf_tensor(f"{tag}_xt", [128, N], fp32))
        self.square_along = ctx.enter_context(nc.sbuf_tensor(f"{tag}_square_along", [128, N], fp32))
        self.square = ctx.enter_context(nc.sbuf_tensor(f"{tag}_square", [128, RT], fp32))


def prepare_gram(nc, sem, tag, rows, gram, root):
    with ExitStack() as ctx:
        ident = ctx.enter_context(nc.sbuf_tensor(f"{tag}g_ident", [128, 128], fp32))
        ones = ctx.enter_context(nc.sbuf_tensor(f"{tag}g_ones", [128, 128], fp32))
        xt2 = ctx.enter_context(nc.sbuf_tensor(f"{tag}g_xt2", [128, N], fp32))
        rows2 = ctx.enter_context(nc.sbuf_tensor(f"{tag}g_rows2", [128, RT, D], fp32))
        turn = ctx.enter_context(nc.psum_tensor(f"{tag}g_turn", [128, 4, 512], fp32))
        spread = ctx.enter_context(nc.psum_tensor(f"{tag}g_spread", [128, 4, 512], fp32))
        ident_made, ones_made, turned = sem(f"{tag}g_ident_made"), sem(f"{tag}g_ones_made"), sem(f"{tag}g_turned")
        copied, squared, spread_done = sem(f"{tag}g_copied"), sem(f"{tag}g_squared"), sem(f"{tag}g_spread_done")
        taken, summed = sem(f"{tag}g_taken"), sem(f"{tag}g_summed")
        pieces = banks(N)
        block = ctx.enter_context(nc.Block())

        @block.gpsimd
        def _(pool):
            write_identity(nc, pool, ident, ident_made)
            pool.memset(ones[:, :], 1.0).then_inc(ones_made, 1)

        @block.tensor
        def _(pe):
            pe.wait_ge(ident_made, 2)
            for b, (a, n) in enumerate(pieces):
                if b >= 4:
                    pe.wait_ge(copied, b - 3)
                for t in range(4 * b, min(4 * b + 4, RT)):
                    w = width(t)
                    mm = pe.transpose(turn[:, b % 4, t % 4 * 128:t % 4 * 128 + w], rows[0:w, t, :],
                                      ident[0:w, 0:w])
                mm.then_inc(turned, 1)
            pe.wait_ge(ones_made, 1)
            for b, (a, n) in enumerate(pieces):
                pe.wait_ge(squared, b + 1)
                if b >= 4:
                    pe.wait_ge(taken, b - 3)
                pe.matmul(spread[:, b % 4, 0:n], ones[:, :], xt2[:, a:a + n], start=True, stop=True) \
                    .then_inc(spread_done, 1)

        @block.vector
        def _(dve):
            for b, (a, n) in enumerate(pieces):
                dve.wait_ge(turned, b + 1)
                dve.tensor_copy(gram.xt[:, a:a + n], turn[:, b % 4, 0:n]).then_inc(copied, 1)
                dve.wait_ge(copied, b + 1)
                dve.tensor_tensor(xt2[:, a:a + n], gram.xt[:, a:a + n], gram.xt[:, a:a + n], ALU.mult) \
                    .then_inc(squared, 1)
            dve.tensor_tensor(rows2[:, :, :], rows[:, :, :], rows[:, :, :], ALU.mult).then_inc(summed, 1)
            dve.wait_ge(summed, 1)
            dve.tensor_reduce(out=gram.square[:, :], in_=rows2[:, :, :], axis=AX.X, op=ALU.add) \
                .then_inc(summed, 1)

        @block.scalar
        def _(act):
            func = ACT.Sqrt if root else ACT.Copy
            for b, (a, n) in enumerate(pieces):
                act.wait_ge(spread_done, b + 1)
                act.activation(gram.square_along[:, a:a + n], spread[:, b % 4, 0:n], func).then_inc(taken, 1)
            if root:
                act.wait_ge(summed, 2)
                act.activation(gram.square[:, :], gram.square[:, :], func).then_inc(taken, 1)


def column_of(buffer, t):
    return buffer[0:width(t), t:t + 1] if isinstance(t, int) else buffer[:, bass.ds(t, 1)]


def ring_free(t, i):
    return t * 7 + (i - 2 if i else 0)


def tile_groups():
    return [[(k, (k - 4 * g) * 128, width(k)) for k in range(4 * g, min(4 * g + 4, RT))]
            for g in range(-(-RT // 4))]


def cosine_attention(nc, sem, adj, beta, gram, x_rows, y_rows):
    pieces, groups = banks(N), tile_groups()
    NP, NG = len(pieces), len(groups)
    with ExitStack() as ctx:
        def sb(name, shape, dt=fp32):
            return ctx.enter_context(nc.sbuf_tensor(name, shape, dt))

        mask = sb("c_mask", [128, 2, N])
        product = sb("c_product", [128, 2, N])
        near_inverse = sb("c_near_inverse", [128, 2, N])
        score = sb("c_score", [128, 2, N])
        own_t = sb("c_own_t", [128, 2, 128])
        own_norm = sb("c_own_norm", [128, 2, 1])
        peak, neg_peak = sb("c_peak", [128, 2, 1]), sb("c_neg_peak", [128, 2, 1])
        weight, inverse = sb("c_weight", [128, 2, 1]), sb("c_inverse", [128, 2, 1])
        score_t = sb("c_score_t", [128, 3, 512])
        beta_in, beta_all = sb("c_beta_in", [1, 1]), sb("c_beta_all", [128, 1])
        ones, ident = sb("c_ones", [1, 128]), sb("c_ident", [128, 128])
        dots = ctx.enter_context(nc.psum_tensor("c_dots", [128, 3, 512], fp32))
        turn = ctx.enter_context(nc.psum_tensor("c_turn", [128, 3, 512], fp32))
        out = ctx.enter_context(nc.psum_tensor("c_out", [128, 2, 512], fp32))
        ident_made, beta_loaded, beta_spread = sem("c_ident_made"), sem("c_beta_loaded"), sem("c_beta_spread")
        zeroed, loaded = sem("c_zeroed"), [sem(f"c_loaded{i}") for i in range(2)]
        own_ready, norm_ready, masked = sem("c_own_ready"), sem("c_norm_ready"), sem("c_masked")
        dotted, divided, steps = sem("c_dotted"), sem("c_divided"), sem("c_steps")
        inverted = sem("c_inverted")
        product_ready, inverse_ready = sem("c_product_ready"), sem("c_inverse_ready")
        probs_ready, turned, emptied = sem("c_probs_ready"), sem("c_turned"), sem("c_emptied")
        multiplied, finished = sem("c_multiplied"), sem("c_finished")
        passed_dve, passed_pool = sem("c_passed_dve"), sem("c_passed_pool")
        DS = 4
        block = ctx.enter_context(nc.Block())

        @block.sync
        def _(sp):
            sp.dma_start(beta_in[:, :], beta.rearrange("(a n) -> a n", a=1)).then_inc(beta_loaded, 16)

            def body(t, p):
                if after(t, 2):
                    sp.wait_ge(steps, t * DS - (DS + 1))
                sp.dma_start(mask[0:width(t), p, :], adj[node_rows(t)]).then_inc(loaded[p], 16)

            tiles(sp, body)

        @block.gpsimd
        def _(pool):
            write_identity(nc, pool, ident, ident_made)
            pool.memset(ones[:, :], 1.0).then_inc(ident_made, 1)

            def body(t, p):
                if after(t, 2):
                    pool.wait_ge(dotted, t * NP - NP)
                    pool.sem_inc(passed_pool, 1)
                pool.tensor_copy(own_t[:, p, 0:width(t)], gram.xt[:, node_rows(t)]).then_inc(own_ready, 1)

            tiles(pool, body)

        @block.tensor
        def _(pe):
            pe.wait_ge(ident_made, 3)
            pe.wait_ge(beta_loaded, 16)
            pe.wait_ge(zeroed, 1)
            pe.matmul(out[:, 0, 0:1], ones[:, :], beta_in[:, :], start=True, stop=True).then_inc(beta_spread, 1)
            pe.wait_ge(beta_spread, 2)

            def dot(t, p):
                pe.wait_ge(own_ready, t + 1)
                for b, (a, w) in enumerate(pieces):
                    if after(t, 1) or b >= 3:
                        pe.wait_ge(divided, ring_free(t, b))
                    pe.matmul(dots[0:width(t), b % 3, 0:w], own_t[:, p, 0:width(t)], gram.xt[:, a:a + w],
                              start=True, stop=True).then_inc(dotted, 1)

            def aggregate(t, p):
                n = width(t)
                pe.wait_ge(probs_ready, t + 1)
                for g in range(NG + 1):
                    if g < NG:
                        if after(t, 1) or g >= 3:
                            pe.wait_ge(emptied, ring_free(t, g))
                        for k, a, w in groups[g]:
                            mm = pe.transpose(turn[0:w, g % 3, a:a + n],
                                              score[0:n, p, k * 128:k * 128 + w], ident[0:n, 0:n])
                        mm.then_inc(turned, 1)
                    if g >= 1:
                        pe.wait_ge(emptied, t * NG + g)
                        if g == 1 and after(t, 2):
                            pe.wait_ge(finished, t)
                        for k, a, w in groups[g - 1]:
                            mm = pe.matmul(out[0:n, p, 0:D], score_t[0:w, (g - 1) % 3, a:a + n],
                                           x_rows[0:w, k, :], start=(k == 0), stop=(k == RT - 1))
                        mm.then_inc(multiplied, 1)

            def body(t, p):
                if not isinstance(t, int) or t < RT:
                    dot(t, p)
                if after(t, 1):
                    aggregate(t - 1, 1 - p)

            tiles(pe, body, end=RT + 1)

        @block.vector
        def _(dve):
            dve.memset(turn[:, :, :].rearrange("p b n -> p (b n)"), 0.0).then_inc(zeroed, 1)
            dve.sem_inc(finished, 1)
            dve.wait_ge(beta_spread, 1)
            dve.tensor_scalar(beta_all[:, :], out[:, 0, 0:1], -1.0, None, ALU.mult).then_inc(beta_spread, 1)
            dve.wait_ge(beta_spread, 2)

            def multiply_norms(t, p):
                n = width(t)
                dve.tensor_copy(own_norm[0:n, p], column_of(gram.square, t)).then_inc(norm_ready, 1)
                dve.wait_ge(norm_ready, t + 1)
                dve.tensor_scalar(product[0:n, p, :], gram.square_along[0:n], own_norm[0:n, p], 1e-7,
                                  ALU.mult, ALU.add).then_inc(product_ready, 1)

            def correct(t, p):
                n, base = width(t), t * DS
                dve.wait_ge(loaded[p], count(t, p))
                dve.tensor_scalar(mask[0:n, p, :], mask[0:n, p, :], 1.0, 1.0e9, ALU.subtract, ALU.mult) \
                    .then_inc(masked, 1)
                dve.wait_ge(inverse_ready, t * 2 + 2)
                dve.tensor_tensor(product[0:n, p, :], product[0:n, p, :], near_inverse[0:n, p, :], ALU.mult) \
                    .then_inc(steps, 1)
                dve.wait_ge(steps, base + 1)
                dve.scalar_tensor_tensor(out=product[0:n, p, :], in0=product[0:n, p, :], scalar=-2.0,
                                         in1=near_inverse[0:n, p, :], op0=ALU.add, op1=ALU.mult) \
                    .then_inc(steps, 1)

            def scores(t, p):
                n, base = width(t), t * DS
                dve.wait_ge(steps, base + 2)
                if after(t, 2):
                    dve.wait_ge(turned, t * NG - NG)
                for b, (a, w) in enumerate(pieces):
                    dve.wait_ge(dotted, t * NP + (b + 1))
                    dve.scalar_tensor_tensor(out=score[0:n, p, a:a + w], in0=dots[0:n, b % 3, 0:w],
                                             scalar=beta_all[0:n], in1=product[0:n, p, a:a + w],
                                             op0=ALU.mult, op1=ALU.mult).then_inc(divided, 1)
                dve.wait_ge(divided, t * NP + NP)
                dve.wait_ge(masked, t + 1)
                dve.sem_inc(passed_dve, 1)
                dve.tensor_tensor_reduce(out=score[0:n, p, :], in0=score[0:n, p, :], in1=mask[0:n, p, :],
                                         scale=1.0, scalar=LOWEST, op0=ALU.add, op1=ALU.max,
                                         accum_out=peak[0:n, p]).then_inc(steps, 1)
                dve.wait_ge(steps, base + 3)
                dve.tensor_scalar(neg_peak[0:n, p], peak[0:n, p], -1.0, None, ALU.mult).then_inc(steps, 1)

            def finish(t, p):
                n = width(t)
                dve.wait_ge(probs_ready, t + 1)
                dve.reciprocal(inverse[0:n, p], weight[0:n, p]).then_inc(inverted, 1)
                dve.wait_ge(multiplied, t * NG + NG)
                dve.wait_ge(inverted, t + 1)
                dve.scalar_tensor_tensor(out=row_of(y_rows, t), in0=out[0:n, p, 0:D], scalar=inverse[0:n, p],
                                         in1=row_of(x_rows, t), op0=ALU.mult, op1=ALU.add).then_inc(finished, 1)

            def body(t, p):
                if not isinstance(t, int) or t < RT - 1:
                    multiply_norms(t + 1, 1 - p)
                if not isinstance(t, int) or t < RT:
                    correct(t, p)
                if after(t, 2):
                    finish(t - 2, p)
                if not isinstance(t, int) or t < RT:
                    scores(t, p)

            multiply_norms(0, 0)
            tiles(dve, body, end=RT + 2)

        @block.scalar
        def _(act):
            def invert(t, p):
                n = width(t)
                act.wait_ge(product_ready, t + 1)
                act.activation(near_inverse[0:n, p, :], product[0:n, p, :], ACT.Ln).then_inc(inverse_ready, 1)
                act.wait_ge(inverse_ready, t * 2 + 1)
                act.activation(near_inverse[0:n, p, :], near_inverse[0:n, p, :], ACT.Exp, scale=-1.0) \
                    .then_inc(inverse_ready, 1)

            def probs(t, p):
                n = width(t)
                act.wait_ge(steps, t * DS + DS)
                act.activation(score[0:n, p, :], score[0:n, p, :], ACT.Exp, bias=neg_peak[0:n, p],
                               accum_out=weight[0:n, p]).then_inc(probs_ready, 1)

            def empty(t):
                for g in range(NG):
                    act.wait_ge(turned, t * NG + (g + 1))
                    if after(t, 1) or g >= 3:
                        act.wait_ge(multiplied, ring_free(t, g))
                    w = 512 if g < NG - 1 else len(groups[g]) * 128
                    act.activation(score_t[:, g % 3, 0:w], turn[:, g % 3, 0:w], ACT.Copy).then_inc(emptied, 1)

            def body(t, p):
                if after(t, 1):
                    probs(t - 1, 1 - p)
                if not isinstance(t, int) or t < RT - 1:
                    invert(t + 1, 1 - p)
                if after(t, 1):
                    empty(t - 1)

            invert(0, 0)
            tiles(act, body, end=RT + 1)


def convolve(nc, sem, tag, matrix, values, W, bias, kind, out_rows, x_rows=None, scale=None, row_sums=None):
    groups = tile_groups()
    NG = len(groups)
    silu = kind in ("silu", "silu_x")
    with ExitStack() as ctx:
        def sb(name, shape, dt=fp32):
            return ctx.enter_context(nc.sbuf_tensor(name, shape, dt))

        rows_in = sb(f"{tag}_rows_in", [128, 2, N])
        matrix_t = sb(f"{tag}_matrix_t", [128, 3, 512])
        hop_t = sb(f"{tag}_hop_t", [128, 2, 128])
        z = sb(f"{tag}_z", [128, 2, D])
        gate = sb(f"{tag}_gate", [128, 2, D])
        own_scale = sb(f"{tag}_own_scale", [128, 2, 1])
        w_in, bias_in, bias_all = sb(f"{tag}_w_in", [128, D]), sb(f"{tag}_bias_in", [1, D]), sb(f"{tag}_bias_all", [128, D])
        ones, ident = sb(f"{tag}_ones", [1, 128]), sb(f"{tag}_ident", [128, 128])
        turn = ctx.enter_context(nc.psum_tensor(f"{tag}_turn", [128, 3, 512], fp32))
        hop = ctx.enter_context(nc.psum_tensor(f"{tag}_hop", [128, 2, 512], fp32))
        mixed = ctx.enter_context(nc.psum_tensor(f"{tag}_mixed", [128, 2, 512], fp32))
        ident_made, w_loaded, bias_spread = sem(f"{tag}_ident_made"), sem(f"{tag}_w_loaded"), sem(f"{tag}_bias_spread")
        loaded = [sem(f"{tag}_loaded{i}") for i in range(2)]
        zeroed, turned, emptied = sem(f"{tag}_zeroed"), sem(f"{tag}_turned"), sem(f"{tag}_emptied")
        multiplied, hop_taken, mixed_done = sem(f"{tag}_multiplied"), sem(f"{tag}_hop_taken"), sem(f"{tag}_mixed_done")
        z_ready, gated, finished = sem(f"{tag}_z_ready"), sem(f"{tag}_gated"), sem(f"{tag}_finished")
        scale_taken, summed, silu_done = sem(f"{tag}_scale_taken"), sem(f"{tag}_summed"), sem(f"{tag}_silu_done")
        passed_sp = sem(f"{tag}_passed_sp")
        block = ctx.enter_context(nc.Block())

        @block.sync
        def _(sp):
            sp.dma_start(w_in[:, :], W).then_inc(w_loaded, 16)
            sp.dma_start(bias_in[:, :], bias.rearrange("(a n) -> a n", a=1)).then_inc(w_loaded, 16)

            def body(t, p):
                if after(t, 2):
                    sp.wait_ge(turned, t * NG - NG)
                    sp.sem_inc(passed_sp, 1)
                    if row_sums is not None:
                        sp.wait_ge(summed, t - 1)
                    sp.sem_inc(passed_sp, 1)
                sp.dma_start(rows_in[0:width(t), p, :], matrix[node_rows(t)]).then_inc(loaded[p], 16)

            tiles(sp, body)

        @block.gpsimd
        def _(pool):
            write_identity(nc, pool, ident, ident_made)
            pool.memset(ones[:, :], 1.0).then_inc(ident_made, 1)

        @block.tensor
        def _(pe):
            pe.wait_ge(ident_made, 3)
            pe.wait_ge(w_loaded, 32)
            pe.wait_ge(zeroed, 1)
            pe.matmul(mixed[:, 0, 0:D], ones[:, :], bias_in[:, :], start=True, stop=True).then_inc(bias_spread, 1)
            pe.wait_ge(bias_spread, 2)

            def mix(t, p):
                pe.wait_ge(hop_taken, t + 1)
                if after(t, 2):
                    pe.wait_ge(z_ready, t)
                pe.matmul(mixed[0:width(t), p, 0:D], hop_t[:, p, 0:width(t)], w_in[:, :],
                          start=True, stop=True).then_inc(mixed_done, 1)

            def body(t, p):
                if isinstance(t, int) and t == RT:
                    mix(t - 1, 1 - p)
                    return
                n = width(t)
                pe.wait_ge(loaded[p], count(t, p))
                for g in range(NG + 1):
                    if g < NG:
                        if after(t, 1) or g >= 3:
                            pe.wait_ge(emptied, ring_free(t, g))
                        for k, a, w in groups[g]:
                            mm = pe.transpose(turn[0:w, g % 3, a:a + n], rows_in[0:n, p, k * 128:k * 128 + w],
                                              ident[0:n, 0:n])
                        mm.then_inc(turned, 1)
                    if g >= 1:
                        pe.wait_ge(emptied, t * NG + g)
                        if g == 1 and after(t, 2):
                            pe.wait_ge(hop_taken, t - 1)
                        for k, a, w in groups[g - 1]:
                            mm = pe.matmul(hop[:, p, 0:n], values[0:w, k, :],
                                           matrix_t[0:w, (g - 1) % 3, a:a + n],
                                           start=(k == 0), stop=(k == RT - 1))
                        mm.then_inc(multiplied, 1)
                    if g == 2 and after(t, 1):
                        mix(t - 1, 1 - p)

            tiles(pe, body, end=RT + 1)

        @block.scalar
        def _(act):
            def gate_tile(t, p):
                act.wait_ge(z_ready, t + 2)
                if after(t, 2):
                    act.wait_ge(finished, t)
                act.activation(gate[0:width(t), p, :], z[0:width(t), p, :], ACT.Sigmoid).then_inc(gated, 1)

            def body(t, p):
                if isinstance(t, int) and t == RT:
                    if silu:
                        gate_tile(t - 1, 1 - p)
                    return
                for g in range(NG):
                    act.wait_ge(turned, t * NG + (g + 1))
                    if after(t, 1) or g >= 3:
                        act.wait_ge(multiplied, ring_free(t, g))
                    w = len(groups[g]) * 128
                    act.activation(matrix_t[:, g % 3, 0:w], turn[:, g % 3, 0:w], ACT.Copy).then_inc(emptied, 1)
                    if g == 4 and silu and after(t, 1):
                        gate_tile(t - 1, 1 - p)

            tiles(act, body, end=RT + 1)

        @block.vector
        def _(dve):
            dve.memset(turn[:, :, :].rearrange("p b n -> p (b n)"), 0.0).then_inc(zeroed, 1)
            dve.sem_inc(z_ready, 1)
            dve.sem_inc(finished, 1)
            dve.wait_ge(bias_spread, 1)
            dve.tensor_copy(bias_all[:, :], mixed[:, 0, 0:D]).then_inc(bias_spread, 1)
            dve.wait_ge(bias_spread, 2)

            def finish(t, p):
                n = width(t)
                if scale is not None:
                    dve.tensor_copy(own_scale[0:n, p], column_of(scale, t)).then_inc(scale_taken, 1)
                    dve.wait_ge(scale_taken, t + 1)
                dve.wait_ge(mixed_done, t + 1)
                if silu:
                    dve.tensor_tensor(z[0:n, p, :], mixed[0:n, p, 0:D], bias_all[0:n, :], ALU.add) \
                        .then_inc(z_ready, 1)
                    dve.wait_ge(gated, t + 1)
                    if kind == "silu":
                        dve.tensor_tensor(row_of(out_rows, t), z[0:n, p, :], gate[0:n, p, :], ALU.mult) \
                            .then_inc(finished, 1)
                        return
                    dve.tensor_tensor(z[0:n, p, :], z[0:n, p, :], gate[0:n, p, :], ALU.mult) \
                        .then_inc(silu_done, 1)
                    dve.wait_ge(silu_done, t + 1)
                else:
                    dve.scalar_tensor_tensor(out=z[0:n, p, :], in0=mixed[0:n, p, 0:D], scalar=own_scale[0:n, p],
                                             in1=bias_all[0:n, :], op0=ALU.mult, op1=ALU.add) \
                        .then_inc(z_ready, 1)
                    dve.wait_ge(z_ready, t + 2)
                if kind == "leaky":
                    dve.scalar_tensor_tensor(out=row_of(out_rows, t), in0=z[0:n, p, :], scalar=0.1,
                                             in1=z[0:n, p, :], op0=ALU.mult, op1=ALU.max).then_inc(finished, 1)
                else:
                    dve.tensor_tensor(row_of(out_rows, t), z[0:n, p, :], row_of(x_rows, t), ALU.add) \
                        .then_inc(finished, 1)

            def body(t, p):
                if isinstance(t, int) and t == RT:
                    finish(t - 1, 1 - p)
                    return
                n = width(t)
                if row_sums is not None:
                    dve.wait_ge(loaded[p], count(t, p))
                    dve.tensor_reduce(out=column_of(row_sums, t), in_=rows_in[0:n, p, :], axis=AX.X,
                                      op=ALU.add).then_inc(summed, 1)
                if after(t, 1):
                    finish(t - 1, 1 - p)
                dve.wait_ge(multiplied, t * NG + NG)
                if after(t, 2):
                    dve.wait_ge(mixed_done, t - 1)
                dve.tensor_copy(hop_t[:, p, 0:n], hop[:, p, 0:n]).then_inc(hop_taken, 1)

            tiles(dve, body, end=RT + 1)


def scale_rows(nc, sem, tag, row_sums, scale, x_rows, scaled):
    with nc.Block() as block:
        rooted, stepped = sem(f"{tag}_rooted"), sem(f"{tag}_stepped")

        @block.scalar
        def _(act):
            act.activation(scale[:, :], row_sums[:, :], ACT.Sqrt).then_inc(rooted, 1)

        @block.vector
        def _(dve):
            dve.wait_ge(rooted, 1)
            dve.reciprocal(scale[:, :], scale[:, :]).then_inc(stepped, 1)
            dve.wait_ge(stepped, 1)
            dve.tensor_tensor(scaled[:, :, :], x_rows[:, :, :],
                              scale[:, :].unsqueeze(2).broadcast_to([128, RT, D]), ALU.mult) \
                .then_inc(stepped, 1)


def nearest_neighbours(nc, sem, adj, gram, graph, row_sums):
    pieces = banks(N)
    NP = len(pieces)
    KEEP, TOP = 4, 8
    with ExitStack() as ctx:
        def sb(name, shape, dt=fp32):
            return ctx.enter_context(nc.sbuf_tensor(name, shape, dt))

        adj_in = sb("s_adj_in", [128, 2, N])
        squares = sb("s_squares", [128, 2, N])
        near = sb("s_near", [128, 2, N + TOP - KEEP])
        others = sb("s_others", [128, N + TOP - KEEP])
        top = sb("s_top", [128, 2, TOP])
        own_t = sb("s_own_t", [128, 2, 128])
        own_square = sb("s_own_square", [128, 2, 1])
        own_sum = sb("s_own_sum", [128, 2, 1])
        dots = ctx.enter_context(nc.psum_tensor("s_dots", [128, 6, 512], fp32))
        loaded = [sem(f"s_loaded{i}") for i in range(2)]
        stored = [sem(f"s_stored{i}") for i in range(2)]
        own_ready, square_ready, squares_ready = sem("s_own_ready"), sem("s_square_ready"), sem("s_squares_ready")
        dotted, subtracted, clamped = sem("s_dotted"), sem("s_subtracted"), sem("s_clamped")
        rooted, near_ready, stepped = sem("s_rooted"), sem("s_near_ready"), sem("s_stepped")
        ends_made, kept, graph_ready = sem("s_ends_made"), sem("s_kept"), sem("s_graph_ready")
        passed_dve, passed_pool = sem("s_passed_dve"), sem("s_passed_pool")
        block = ctx.enter_context(nc.Block())

        @block.sync
        def _(sp):
            def store(t, p):
                sp.wait_ge(graph_ready, t + 1)
                sp.dma_start(graph[node_rows(t)], adj_in[0:width(t), p, :]).then_inc(stored[p], 16)

            def body(t, p):
                if after(t, 2):
                    store(t - 2, p)
                    sp.wait_ge(stored[p], count(t - 2, p))
                sp.dma_start(adj_in[0:width(t), p, :], adj[node_rows(t)]).then_inc(loaded[p], 16)

            tiles(sp, body)
            for p in range(2):
                store(RT - 2 + p, p)
                sp.wait_ge(stored[p], 16 * RT // 2)

        @block.gpsimd
        def _(pool):
            def body(t, p):
                n = width(t)
                if after(t, 2):
                    pool.wait_ge(dotted, t * NP - NP)
                    pool.sem_inc(passed_pool, 1)
                pool.tensor_copy(own_t[:, p, 0:n], gram.xt[:, node_rows(t)]).then_inc(own_ready, 1)

            tiles(pool, body)

        @block.tensor
        def _(pe):
            def body(t, p):
                n = width(t)
                pe.wait_ge(own_ready, t + 1)
                for b, (a, w) in enumerate(pieces):
                    if b == 6:
                        pe.wait_ge(subtracted, t * NP + 1)
                    elif after(t, 1):
                        pe.wait_ge(subtracted, t * NP - (0 if b == 0 else NP - 1 - b))
                    pe.matmul(dots[0:n, b % 6, 0:w], own_t[:, p, 0:n], gram.xt[:, a:a + w],
                              start=True, stop=True).then_inc(dotted, 1)

            tiles(pe, body)

        @block.scalar
        def _(act):
            def add_squares(t, p):
                n = width(t)
                act.wait_ge(square_ready, t + 1)
                if after(t, 2):
                    act.wait_ge(subtracted, t * NP - NP)
                act.activation(squares[0:n, p, :], gram.square_along[0:n, :], ACT.Identity,
                               bias=own_square[0:n, p]).then_inc(squares_ready, 1)

            def body(t, p):
                n = width(t)
                act.wait_ge(clamped, t + 1)
                act.activation(near[0:n, p, 0:N], near[0:n, p, 0:N], ACT.Sqrt).then_inc(rooted, 1)
                act.wait_ge(rooted, t + 1)
                act.activation(near[0:n, p, 0:N], near[0:n, p, 0:N], ACT.Exp, scale=-0.5) \
                    .then_inc(near_ready, 1)
                if not isinstance(t, int) or t < RT - 1:
                    add_squares(t + 1, 1 - p)

            add_squares(0, 0)
            tiles(act, body)

        @block.vector
        def _(dve):
            for p in range(2):
                dve.memset(near[:, p, N:], -1.0).then_inc(ends_made, 1)
            dve.wait_ge(ends_made, 2)

            def take_square(t, p):
                dve.tensor_copy(own_square[0:width(t), p], column_of(gram.square, t)).then_inc(square_ready, 1)

            def distances(t, p):
                n = width(t)
                dve.wait_ge(squares_ready, t + 1)
                if not isinstance(t, int) or t < RT - 1:
                    take_square(t + 1, 1 - p)
                for b, (a, w) in enumerate(pieces):
                    dve.wait_ge(dotted, t * NP + (b + 1))
                    dve.scalar_tensor_tensor(out=near[0:n, p, a:a + w], in0=dots[0:n, b % 6, 0:w], scalar=-2.0,
                                             in1=squares[0:n, p, a:a + w], op0=ALU.mult, op1=ALU.add) \
                        .then_inc(subtracted, 1)
                dve.wait_ge(subtracted, t * NP + NP)
                dve.tensor_scalar(near[0:n, p, 0:N], near[0:n, p, 0:N], 0.0, 1e-10, ALU.max, ALU.add) \
                    .then_inc(clamped, 1)

            def keep(t, p):
                n, base = width(t), t * 5
                dve.wait_ge(near_ready, t + 1)
                dve.sem_inc(passed_dve, 1)
                dve.max(top[0:n, p, :], near[0:n, p, 0:N]).then_inc(stepped, 1)
                dve.wait_ge(stepped, base + 1)
                dve.sem_inc(passed_dve, 1)
                dve.memset(top[0:n, p, KEEP:], -1.0).then_inc(stepped, 1)
                dve.wait_ge(stepped, base + 2)
                dve.sem_inc(passed_dve, 1)
                dve.match_replace(others[0:n, :], top[0:n, p, :], near[0:n, p, :], 0.0).then_inc(stepped, 1)
                dve.wait_ge(stepped, base + 3)
                dve.tensor_tensor(near[0:n, p, 0:N], near[0:n, p, 0:N], others[0:n, 0:N], ALU.subtract) \
                    .then_inc(stepped, 1)
                dve.wait_ge(loaded[p], count(t, p))
                dve.wait_ge(stepped, base + 4)
                dve.sem_inc(passed_dve, 1)
                dve.tensor_tensor_reduce(out=adj_in[0:n, p, :], in0=near[0:n, p, 0:N], in1=adj_in[0:n, p, :],
                                         scale=1.0, scalar=0.0, op0=ALU.add, op1=ALU.add,
                                         accum_out=own_sum[0:n, p]).then_inc(graph_ready, 1)
                dve.wait_ge(graph_ready, t + 1)
                dve.tensor_copy(column_of(row_sums, t), own_sum[0:n, p]).then_inc(stepped, 1)

            def body(t, p):
                if not isinstance(t, int) or t < RT:
                    distances(t, p)
                if after(t, 1):
                    keep(t - 1, 1 - p)

            take_square(0, 0)
            tiles(dve, body, end=RT + 1)


def store_output(nc, sem, x_rows, out):
    stored = sem("o_stored")
    with nc.Block() as block:
        @block.sync
        def _(sp):
            sp.dma_start(out[0:128 * (RT - 1)].rearrange("(t p) d -> p t d", p=128),
                         x_rows[:, 0:RT - 1, :]).then_inc(stored, 16)
            sp.dma_start(out[128 * (RT - 1):N], x_rows[0:LAST, RT - 1, :]).then_inc(stored, 16)
            sp.wait_ge(stored, 32)


def stage(nc, build, *args, **kwargs):
    held = []

    def sem(name):
        held.append(nc.alloc_semaphore(name))
        return held[-1]

    build(nc, sem, *args, **kwargs)
    nc.clear_and_free_semaphores(held)
    nc.all_engine_barrier()


def four_layers(nc, x, adj, Wq, Wk, Wv, Wo, beta, W2, b2, W3a, b3a, W3b, b3b, out, debug=None):
    def dram(name, shape, dt=fp32):
        return nc.dram_tensor(name, shape, dt, kind=(debug or {}).get(name, "Internal")).ap()

    q_planes, k_planes = dram("q_planes", [3, C, G], bf16), dram("k_planes", [3, C, G], bf16)
    v_planes, v_tiles = dram("v_planes", [C, G]), dram("v_tiles", [HEADS, 128, V_ROW])
    sum_planes = dram("sum_planes", [C + 1, G])
    graph = dram("graph", [N, N])

    stage(nc, project, x, Wq, Wk, Wv, q_planes, k_planes, v_planes)
    stage(nc, lay_out_values, v_planes, v_tiles)
    stage(nc, attention, adj, q_planes, k_planes, v_tiles, sum_planes)
    with ExitStack() as ctx:
        x_rows, y_rows, hidden = (ctx.enter_context(nc.sbuf_tensor(name, [128, RT, D], fp32))
                                  for name in ("x_rows", "y_rows", "hidden"))
        row_sums, scale = (ctx.enter_context(nc.sbuf_tensor(name, [128, RT], fp32))
                           for name in ("row_sums", "scale"))
        stage(nc, join_heads, x, sum_planes, Wo, x_rows, y_rows)
        stage(nc, layer_norm, "norm0", y_rows, x_rows)
        with ExitStack() as inner:
            gram = Gram(nc, inner, "x")
            stage(nc, prepare_gram, "x", x_rows, gram, True)
            stage(nc, cosine_attention, adj, beta, gram, x_rows, y_rows)
        stage(nc, layer_norm, "norm1", y_rows, x_rows)
        stage(nc, clear_sums, row_sums, hidden)
        stage(nc, convolve, "hop1", adj, x_rows, W2, b2, "silu", hidden, row_sums=row_sums)
        stage(nc, convolve, "hop2", adj, hidden, W2, b2, "silu_x", y_rows, x_rows=x_rows)
        stage(nc, layer_norm, "norm2", y_rows, x_rows)
        stage(nc, scale_rows, "degree1", row_sums, scale, x_rows, y_rows)
        stage(nc, convolve, "lap1", adj, y_rows, W3a, b3a, "leaky", hidden, scale=scale)
        with ExitStack() as inner:
            gram = Gram(nc, inner, "z")
            stage(nc, prepare_gram, "z", hidden, gram, False)
            stage(nc, nearest_neighbours, adj, gram, graph, row_sums)
        stage(nc, scale_rows, "degree2", row_sums, scale, x_rows, hidden)
        stage(nc, convolve, "lap2", graph, hidden, W3b, b3b, "scaled", y_rows, x_rows=x_rows, scale=scale)
        stage(nc, layer_norm, "norm3", y_rows, x_rows)
        stage(nc, store_output, x_rows, out)


def clear_sums(nc, sem, row_sums, hidden):
    cleared = sem("z_cleared")
    with nc.Block() as block:
        @block.vector
        def _(dve):
            dve.memset(row_sums[:, :], 1.0).then_inc(cleared, 1)
            dve.memset(hidden[:, :, :].rearrange("p t d -> p (t d)"), 0.0).then_inc(cleared, 1)


_INS = ["x", "adj", "L0_gnn_Wq", "L0_gnn_Wk", "L0_gnn_Wv", "L0_gnn_Wo", "L1_gnn_beta", "L2_gnn_W", "L2_gnn_b",
        "L3_gnn_W1", "L3_gnn_b1", "L3_gnn_W2", "L3_gnn_b2"]


def kernel(**inputs):
    import numpy as _np
    import concourse.bacc as _bacc
    from concourse import mybir as _mybir
    from concourse.bass_utils import run_bass_kernel_spmd as _run

    nc = _bacc.Bacc("TRN2", target_bir_lowering=False, num_devices=1)
    arrays, args = {}, []
    for name in _INS:
        a = _np.ascontiguousarray(inputs[name])
        arrays[f"in_{name}_dram"] = a
        args.append(nc.dram_tensor(f"in_{name}_dram", a.shape, _mybir.dt.from_np(a.dtype),
                                   kind="ExternalInput").ap())
    out = nc.dram_tensor("out_0_dram", (N, D), _mybir.dt.float32, kind="ExternalOutput").ap()
    four_layers(nc, *args, out)
    return _run(nc, [arrays], core_ids=[0]).results[0]["out_0_dram"]
```
